# Optimizing a Trainium2 kernel written in Bass

```python
import numpy as np
import jax
import jax.numpy as jnp

def _softmax(x, axis=-1):
    return jax.nn.softmax(x, axis=axis)

def _gelu(x):
    return jax.nn.gelu(x, approximate=True)

def _silu(x):
    return jax.nn.silu(x)

def _sigmoid(x):
    return jax.nn.sigmoid(x)

def _layernorm(x, axis=-1, eps=1e-05):
    m = jnp.mean(x, axis=axis, keepdims=True)
    v = jnp.var(x, axis=axis, keepdims=True)
    return (x - m) / jnp.sqrt(v + eps)

def _scatter_add(tgt, idx, src, axis=0):
    return tgt.at[idx].add(src)

def _segment_sum(src, seg, n):
    return jax.ops.segment_sum(src, seg, n)
kernel_name = 'mk_cond_seq_d2_seqx_r4_d169eb'

def setup_inputs(seed: int=0):
    np.random.seed(seed)
    _w = jnp.asarray

    def _rec_inputs():
        import jax
        import jax.numpy as jnp
        _rk = jax.random.key(seed)
        x = -0.0002928 + 1 * jax.random.normal(jax.random.fold_in(_rk, 1), (4, 512, 256), jnp.float32)
        _lenS = 512 - jax.random.randint(jax.random.fold_in(_rk, 7), (4,), 0, max(1, 512 // 4) + 1, jnp.int32)
        _lenS2 = 512 - jax.random.randint(jax.random.fold_in(_rk, 8), (4,), 0, max(1, 512 // 4) + 1, jnp.int32)
        cond_1024 = 0.000887014 + 1.03683 * jax.random.normal(jax.random.fold_in(_rk, 11), (4, 256), jnp.float32)
        return (x, cond_1024)
    x, cond_1024 = _rec_inputs()

    def _L0_cond_setup():
        import jax, jax.numpy as jnp
        import numpy as np
        B, L, D_MODEL, COND = (2, 512, 256, 256)
        D_STATE, EXPAND = (64, 2)
        D_INNER = EXPAND * D_MODEL
        MLP_H = 2 * D_MODEL
        EPS = 1e-05

        def _adaln(x, c, w, b):
            mod = (c @ w + b)[:, None, :]
            shift, scale, gate = jnp.split(mod, 3, axis=-1)
            mu = jnp.mean(x, axis=-1, keepdims=True)
            var = jnp.var(x, axis=-1, keepdims=True)
            normed = (x - mu) * jax.lax.rsqrt(var + EPS) * (1.0 + scale) + shift
            return (normed, gate)

        def _ssm(h, in_w, xproj_w, dt_bias, A_log, Dskip, out_w):
            xz = h @ in_w
            xs, z = jnp.split(xz, 2, axis=-1)
            xs = jax.nn.silu(xs)
            proj = xs @ xproj_w
            dt = jax.nn.softplus(proj[..., :D_INNER] + dt_bias)
            Bm = proj[..., D_INNER:D_INNER + D_STATE]
            Cm = proj[..., D_INNER + D_STATE:]
            A = -jnp.exp(A_log)

            def step(hst, ins):
                dt_t, B_t, C_t, x_t = ins
                dA = jnp.exp(dt_t[:, :, None] * A)
                hst = hst * dA + (dt_t * x_t)[:, :, None] * B_t[:, None, :]
                y_t = jnp.einsum('bds,bs->bd', hst, C_t)
                return (hst, y_t)
            tm = lambda a: jnp.swapaxes(a, 0, 1)
            h0 = jnp.zeros((h.shape[0], D_INNER, D_STATE), h.dtype)
            _, ys = jax.lax.scan(step, h0, (tm(dt), tm(Bm), tm(Cm), tm(xs)))
            y = jnp.swapaxes(ys, 0, 1) + xs * Dskip
            return y * jax.nn.silu(z) @ out_w
        key = jax.random.key(seed)
        ks = jax.random.split(key, 24)
        p = lambda i, shape, s=0.02: jax.random.normal(ks[i], shape, jnp.float32) * s
        inp = {'x': jax.random.normal(ks[0], (B, L, D_MODEL), jnp.float32), 'c': jax.random.normal(ks[1], (B, COND), jnp.float32), 'adaln_mamba_w': p(2, (COND, 3 * D_MODEL)), 'adaln_mamba_b': jnp.zeros((3 * D_MODEL,), jnp.float32), 'adaln_mlp_w': p(3, (COND, 3 * D_MODEL)), 'adaln_mlp_b': jnp.zeros((3 * D_MODEL,), jnp.float32), 'mlp_w1': p(4, (D_MODEL, MLP_H)), 'mlp_w2': p(5, (D_MODEL, MLP_H)), 'mlp_w3': p(6, (MLP_H, D_MODEL))}
        a_init = jnp.log(jnp.tile(jnp.arange(1, D_STATE + 1, dtype=jnp.float32), (D_INNER, 1)))
        for j, pre in enumerate(['fwd', 'bwd']):
            o = 7 + 6 * j
            inp[f'{pre}_in_w'] = p(o, (D_MODEL, 2 * D_INNER))
            inp[f'{pre}_xproj_w'] = p(o + 1, (D_INNER, D_INNER + 2 * D_STATE))
            inp[f'{pre}_dt_bias'] = jnp.zeros((D_INNER,), jnp.float32)
            inp[f'{pre}_A_log'] = a_init
            inp[f'{pre}_D'] = jnp.ones((D_INNER,), jnp.float32)
            inp[f'{pre}_out_w'] = p(o + 2, (D_INNER, D_MODEL))
        return inp
    _L0_cond_all = _L0_cond_setup()
    _L0_cond_in = {k: v for k, v in _L0_cond_all.items() if k in ('adaln_mamba_w', 'adaln_mamba_b', 'adaln_mlp_w', 'adaln_mlp_b', 'mlp_w1', 'mlp_w2', 'mlp_w3', 'fwd_in_w', 'fwd_xproj_w', 'fwd_dt_bias', 'fwd_A_log', 'fwd_D', 'fwd_out_w', 'bwd_in_w', 'bwd_xproj_w', 'bwd_dt_bias', 'bwd_A_log', 'bwd_D', 'bwd_out_w')}
    del _L0_cond_all

    def _L1_cond_setup():
        import jax, jax.numpy as jnp
        import numpy as np
        EPS_LN = 1e-06
        EPS_NORM = 1e-12
        MAX_SCALE_MUL = float(np.log(100.0))
        H = 16

        def _ln(x):
            mu = jnp.mean(x, axis=-1, keepdims=True)
            var = jnp.mean((x - mu) ** 2, axis=-1, keepdims=True)
            return (x - mu) / jnp.sqrt(var + EPS_LN)

        def _l2norm(x):
            n = jnp.sqrt(jnp.sum(x * x, axis=-1, keepdims=True))
            return x / jnp.maximum(n, EPS_NORM)
        key = jax.random.key(seed)
        ks = jax.random.split(key, 12)
        B, L, C = (4, 256, 256)
        Ccond, Dff = (256, 1024)
        s = lambda fan: 1.0 / np.sqrt(fan)
        return {'x': jax.random.normal(ks[0], (B, L, C), jnp.float32), 'cond': jax.random.normal(ks[1], (B, Ccond), jnp.float32), 'mat_qkv_w': jax.random.normal(ks[2], (3 * C, C), jnp.float32) * s(C), 'q_bias': jnp.zeros((C,), jnp.float32), 'v_bias': jnp.zeros((C,), jnp.float32), 'scale_mul': jnp.full((1, H, 1, 1), np.log(4.0), jnp.float32), 'proj_w': jax.random.normal(ks[3], (C, C), jnp.float32) * s(C), 'proj_b': jnp.zeros((C,), jnp.float32), 'ada_w': jax.random.normal(ks[4], (6 * C, Ccond), jnp.float32) * s(Ccond), 'ada_b': jnp.zeros((6 * C,), jnp.float32), 'fc1_w': jax.random.normal(ks[5], (Dff, C), jnp.float32) * s(C), 'fc1_b': jnp.zeros((Dff,), jnp.float32), 'fc2_w': jax.random.normal(ks[6], (C, Dff), jnp.float32) * s(Dff), 'fc2_b': jnp.zeros((C,), jnp.float32)}
    _L1_cond_all = _L1_cond_setup()
    _L1_cond_in = {k: v for k, v in _L1_cond_all.items() if k in ('mat_qkv_w', 'q_bias', 'v_bias', 'scale_mul', 'proj_w', 'proj_b', 'ada_w', 'ada_b', 'fc1_w', 'fc1_b', 'fc2_w', 'fc2_b')}
    del _L1_cond_all
    return {'x': x, 'cond_1024': cond_1024, 'L0_cond_adaln_mamba_w': _L0_cond_in['adaln_mamba_w'], 'L0_cond_adaln_mamba_b': _L0_cond_in['adaln_mamba_b'], 'L0_cond_adaln_mlp_w': _L0_cond_in['adaln_mlp_w'], 'L0_cond_adaln_mlp_b': _L0_cond_in['adaln_mlp_b'], 'L0_cond_mlp_w1': _L0_cond_in['mlp_w1'], 'L0_cond_mlp_w2': _L0_cond_in['mlp_w2'], 'L0_cond_mlp_w3': _L0_cond_in['mlp_w3'], 'L0_cond_fwd_in_w': _L0_cond_in['fwd_in_w'], 'L0_cond_fwd_xproj_w': _L0_cond_in['fwd_xproj_w'], 'L0_cond_fwd_dt_bias': _L0_cond_in['fwd_dt_bias'], 'L0_cond_fwd_A_log': _L0_cond_in['fwd_A_log'], 'L0_cond_fwd_D': _L0_cond_in['fwd_D'], 'L0_cond_fwd_out_w': _L0_cond_in['fwd_out_w'], 'L0_cond_bwd_in_w': _L0_cond_in['bwd_in_w'], 'L0_cond_bwd_xproj_w': _L0_cond_in['bwd_xproj_w'], 'L0_cond_bwd_dt_bias': _L0_cond_in['bwd_dt_bias'], 'L0_cond_bwd_A_log': _L0_cond_in['bwd_A_log'], 'L0_cond_bwd_D': _L0_cond_in['bwd_D'], 'L0_cond_bwd_out_w': _L0_cond_in['bwd_out_w'], 'L1_cond_mat_qkv_w': _L1_cond_in['mat_qkv_w'], 'L1_cond_q_bias': _L1_cond_in['q_bias'], 'L1_cond_v_bias': _L1_cond_in['v_bias'], 'L1_cond_scale_mul': _L1_cond_in['scale_mul'], 'L1_cond_proj_w': _L1_cond_in['proj_w'], 'L1_cond_proj_b': _L1_cond_in['proj_b'], 'L1_cond_ada_w': _L1_cond_in['ada_w'], 'L1_cond_ada_b': _L1_cond_in['ada_b'], 'L1_cond_fc1_w': _L1_cond_in['fc1_w'], 'L1_cond_fc1_b': _L1_cond_in['fc1_b'], 'L1_cond_fc2_w': _L1_cond_in['fc2_w'], 'L1_cond_fc2_b': _L1_cond_in['fc2_b']}

def reference(x, cond_1024, L0_cond_adaln_mamba_w, L0_cond_adaln_mamba_b, L0_cond_adaln_mlp_w, L0_cond_adaln_mlp_b, L0_cond_mlp_w1, L0_cond_mlp_w2, L0_cond_mlp_w3, L0_cond_fwd_in_w, L0_cond_fwd_xproj_w, L0_cond_fwd_dt_bias, L0_cond_fwd_A_log, L0_cond_fwd_D, L0_cond_fwd_out_w, L0_cond_bwd_in_w, L0_cond_bwd_xproj_w, L0_cond_bwd_dt_bias, L0_cond_bwd_A_log, L0_cond_bwd_D, L0_cond_bwd_out_w, L1_cond_mat_qkv_w, L1_cond_q_bias, L1_cond_v_bias, L1_cond_scale_mul, L1_cond_proj_w, L1_cond_proj_b, L1_cond_ada_w, L1_cond_ada_b, L1_cond_fc1_w, L1_cond_fc1_b, L1_cond_fc2_w, L1_cond_fc2_b):
    import jax
    import jax.numpy as jnp

    def _L0_cond_ref(x, c, adaln_mamba_w, adaln_mamba_b, adaln_mlp_w, adaln_mlp_b, mlp_w1, mlp_w2, mlp_w3, fwd_in_w, fwd_xproj_w, fwd_dt_bias, fwd_A_log, fwd_D, fwd_out_w, bwd_in_w, bwd_xproj_w, bwd_dt_bias, bwd_A_log, bwd_D, bwd_out_w):
        import jax, jax.numpy as jnp
        import numpy as np
        B, L, D_MODEL, COND = (2, 512, 256, 256)
        D_STATE, EXPAND = (64, 2)
        D_INNER = EXPAND * D_MODEL
        MLP_H = 2 * D_MODEL
        EPS = 1e-05

        def _adaln(x, c, w, b):
            mod = (c @ w + b)[:, None, :]
            shift, scale, gate = jnp.split(mod, 3, axis=-1)
            mu = jnp.mean(x, axis=-1, keepdims=True)
            var = jnp.var(x, axis=-1, keepdims=True)
            normed = (x - mu) * jax.lax.rsqrt(var + EPS) * (1.0 + scale) + shift
            return (normed, gate)

        def _ssm(h, in_w, xproj_w, dt_bias, A_log, Dskip, out_w):
            xz = h @ in_w
            xs, z = jnp.split(xz, 2, axis=-1)
            xs = jax.nn.silu(xs)
            proj = xs @ xproj_w
            dt = jax.nn.softplus(proj[..., :D_INNER] + dt_bias)
            Bm = proj[..., D_INNER:D_INNER + D_STATE]
            Cm = proj[..., D_INNER + D_STATE:]
            A = -jnp.exp(A_log)

            def step(hst, ins):
                dt_t, B_t, C_t, x_t = ins
                dA = jnp.exp(dt_t[:, :, None] * A)
                hst = hst * dA + (dt_t * x_t)[:, :, None] * B_t[:, None, :]
                y_t = jnp.einsum('bds,bs->bd', hst, C_t)
                return (hst, y_t)
            tm = lambda a: jnp.swapaxes(a, 0, 1)
            h0 = jnp.zeros((h.shape[0], D_INNER, D_STATE), h.dtype)
            _, ys = jax.lax.scan(step, h0, (tm(dt), tm(Bm), tm(Cm), tm(xs)))
            y = jnp.swapaxes(ys, 0, 1) + xs * Dskip
            return y * jax.nn.silu(z) @ out_w
        h, gate = _adaln(x, c, adaln_mamba_w, adaln_mamba_b)
        h_fwd = _ssm(h, fwd_in_w, fwd_xproj_w, fwd_dt_bias, fwd_A_log, fwd_D, fwd_out_w)
        h_bwd = jnp.flip(_ssm(jnp.flip(h, 1), bwd_in_w, bwd_xproj_w, bwd_dt_bias, bwd_A_log, bwd_D, bwd_out_w), 1)
        x = x + gate * (h_fwd + h_bwd)
        h, gate = _adaln(x, c, adaln_mlp_w, adaln_mlp_b)
        mlp_out = jax.nn.silu(h @ mlp_w1) * (h @ mlp_w2) @ mlp_w3
        return x + gate * mlp_out

    def _L1_cond_ref(x, cond, mat_qkv_w, q_bias, v_bias, scale_mul, proj_w, proj_b, ada_w, ada_b, fc1_w, fc1_b, fc2_w, fc2_b):
        import jax, jax.numpy as jnp
        import numpy as np
        EPS_LN = 1e-06
        EPS_NORM = 1e-12
        MAX_SCALE_MUL = float(np.log(100.0))
        H = 16

        def _ln(x):
            mu = jnp.mean(x, axis=-1, keepdims=True)
            var = jnp.mean((x - mu) ** 2, axis=-1, keepdims=True)
            return (x - mu) / jnp.sqrt(var + EPS_LN)

        def _l2norm(x):
            n = jnp.sqrt(jnp.sum(x * x, axis=-1, keepdims=True))
            return x / jnp.maximum(n, EPS_NORM)
        B, L, C = x.shape
        hd = C // H
        ada = jax.nn.silu(cond) @ ada_w.T + ada_b
        ada = ada.reshape(B, 1, 6, C)
        gamma1, gamma2, scale1, scale2, shift1, shift2 = [ada[:, :, i] for i in range(6)]
        x1 = _ln(x) * (scale1 + 1.0) + shift1
        qkv_bias = jnp.concatenate([q_bias, jnp.zeros_like(q_bias), v_bias])
        qkv = (x1 @ mat_qkv_w.T + qkv_bias).reshape(B, L, 3, H, hd)
        q, k, v = [jnp.transpose(qkv[:, :, i], (0, 2, 1, 3)) for i in range(3)]
        sm = jnp.exp(jnp.minimum(scale_mul, MAX_SCALE_MUL))
        q = _l2norm(q) * sm
        k = _l2norm(k)
        scores = jnp.einsum('bhqd,bhkd->bhqk', q, k)
        probs = jax.nn.softmax(scores, axis=-1)
        o = jnp.einsum('bhqk,bhkd->bhqd', probs, v)
        o = jnp.transpose(o, (0, 2, 1, 3)).reshape(B, L, C)
        attn_out = o @ proj_w.T + proj_b
        x = x + attn_out * gamma1
        x2 = _ln(x) * (scale2 + 1.0) + shift2
        h = jax.nn.gelu(x2 @ fc1_w.T + fc1_b, approximate=False)
        ffn_out = h @ fc2_w.T + fc2_b
        x = x + ffn_out * gamma2
        return x
    x = _L0_cond_ref(x, cond_1024, L0_cond_adaln_mamba_w, L0_cond_adaln_mamba_b, L0_cond_adaln_mlp_w, L0_cond_adaln_mlp_b, L0_cond_mlp_w1, L0_cond_mlp_w2, L0_cond_mlp_w3, L0_cond_fwd_in_w, L0_cond_fwd_xproj_w, L0_cond_fwd_dt_bias, L0_cond_fwd_A_log, L0_cond_fwd_D, L0_cond_fwd_out_w, L0_cond_bwd_in_w, L0_cond_bwd_xproj_w, L0_cond_bwd_dt_bias, L0_cond_bwd_A_log, L0_cond_bwd_D, L0_cond_bwd_out_w)
    x = _L1_cond_ref(x, cond_1024, L1_cond_mat_qkv_w, L1_cond_q_bias, L1_cond_v_bias, L1_cond_scale_mul, L1_cond_proj_w, L1_cond_proj_b, L1_cond_ada_w, L1_cond_ada_b, L1_cond_fc1_w, L1_cond_fc1_b, L1_cond_fc2_w, L1_cond_fc2_b)
    return x

_drawn_inputs = setup_inputs


def setup_inputs(seed=0):
    import zlib

    import numpy as np

    out = dict(_drawn_inputs(seed))
    spreads = {'L0_cond_adaln_mamba_b': (0.0, 0.1),
     'L0_cond_adaln_mlp_b': (0.0, 0.1),
     'L0_cond_fwd_dt_bias': (0.0, 0.1),
     'L0_cond_fwd_D': (1.0, 0.2),
     'L0_cond_bwd_dt_bias': (0.0, 0.1),
     'L0_cond_bwd_D': (1.0, 0.2),
     'L1_cond_q_bias': (0.0, 0.1),
     'L1_cond_v_bias': (0.0, 0.1),
     'L1_cond_scale_mul': (1.3862943649291992, 0.2),
     'L1_cond_proj_b': (0.0, 0.1),
     'L1_cond_ada_b': (0.0, 0.1),
     'L1_cond_fc1_b': (0.0, 0.1),
     'L1_cond_fc2_b': (0.0, 0.1)}
    factors = {}
    for name, (base, spread) in spreads.items():
        noise = np.random.default_rng([zlib.crc32(name.encode()), seed]).standard_normal(out[name].shape)
        drawn = base * np.exp(spread * noise) if base else spread * noise
        out[name] = jnp.asarray(drawn.astype(out[name].dtype))
    for name, factor in factors.items():
        out[name] = (out[name] * factor).astype(out[name].dtype)
    return out
```

```python
from contextlib import ExitStack

import concourse.bass as bass
from concourse import mybir

F32 = mybir.dt.float32
BF16 = mybir.dt.bfloat16
ALU = mybir.AluOpType
ACT = mybir.ActivationFunctionType
AX = mybir.AxisListType

P = 128
B = 4
L = 512
D = 256
DI = 512
NS = 64
HID = 512
FF = 1024
H = 16
HD = D // H
TT = L // P
KD = D // P
KI = DI // P
KH = HID // P
KF = FF // P
LANE = 32
HG = P // LANE
NG = H // HG
VW = HD + 1
RING = 4
CREDIT = RING + 1
EPS_MAMBA = 1e-5
EPS_LN = 1e-6
EPS_NORM = 1e-12
MAX_SCALE_MUL = 4.605170185988092
SHIFT, SCALE = 0, 1
GATE_MAMBA, GATE_MLP, GAMMA1, GAMMA2 = range(4)
Q_BIAS, V_BIAS, PROJ_B, FC2_B = range(4)

INPUTS = {
    "x": [B, L, D],
    "cond": [P, KD, B],
    "mod_w": [P, KD, 4, 2, D],
    "mod_b": [P, 4, 2, KD],
    "gate_w": [P, KD, 4, D],
    "gate_b": [4, D],
    "in_w": [2, P, KD, 2 * DI],
    "xproj_w": [2, P, KI, DI + 2 * NS],
    "dt_b": [P, 2, KI],
    "a_log": [P, 2, KI, NS],
    "d_skip": [P, 2, KI],
    "out_w": [P, 2, KI, D],
    "w12": [P, 2, KD, HID],
    "w3": [P, KH, D],
    "qkv_w": [P, KD, 3 * D],
    "row_b": [4, D],
    "scale_mul": [1, H],
    "proj_w": [P, KD, D],
    "fc1_w": [P, KD, FF],
    "fc1_b": [P, KF],
    "fc2_w": [P, KF, D],
}


def build(nc, inp, out):
    ctx = ExitStack()
    with ctx:
        def sb(name, shape, dtype=F32):
            return ctx.enter_context(nc.sbuf_tensor(name, shape, dtype))

        def sem(name):
            return ctx.enter_context(nc.semaphore(name))

        ident = sb("ident", [P, P])
        ident_bf = sb("ident_bf", [P, P], BF16)
        cond = sb("cond", [P, KD, B])
        silu_cond = sb("silu_cond", [P, KD, B])
        mod_b = sb("mod_b", [P, 4, 2, KD])
        mod = sb("mod", [P, 4, 2, KD, B])
        gate = sb("gate", [P, B, 4, D])
        in_w0 = sb("in_w0", [P, KD, 2 * DI])
        in_w1 = sb("in_w1", [P, KD, 2 * DI])
        in_w = [in_w0, in_w1]
        fc1_w = in_w0
        xproj_w0 = sb("xproj_w0", [P, KI, DI + 2 * NS])
        xproj_w1 = sb("xproj_w1", [P, KI, DI + 2 * NS])
        xproj_w = [xproj_w0, xproj_w1]
        w12 = xproj_w0[:].rearrange("p k n -> p (k n)")[:, 0:2 * KD * HID].rearrange("p (w k n) -> p w k n", w=2, k=KD)
        dt_b = sb("dt_b", [P, 2, KI])
        a_log = sb("a_log", [P, 2, KI, NS])
        a_exp = sb("a_exp", [P, 2, KI, NS])
        a_neg = sb("a_neg", [P, 2, KI, NS])
        d_skip = sb("d_skip", [P, 2, KI])
        d_diag = sb("d_diag", [P, 2, KI, P])
        out_w = sb("out_w", [P, 2, KI, D])
        w3 = sb("w3", [P, KH, D])
        qkv_w = sb("qkv_w", [P, KD, 3 * D])
        row_b = sb("row_b", [P, 4, D])
        scale_mul = sb("scale_mul", [P, H])
        scale_cap = sb("scale_cap", [P, H])
        q_scale = sb("q_scale", [P, H])
        proj_w = sb("proj_w", [P, KD, D])
        fc1_b = sb("fc1_b", [P, KF])
        fc2_w = sb("fc2_w", [P, KF, D])

        x_in = sb("x_in", [P, TT, D])
        x_ssm = sb("x_ssm", [P, TT, D])
        x_mlp = sb("x_mlp", [P, TT, D])
        x_att = x_ssm
        x_out = x_mlp
        stats = sb("stats", [P, TT, 6])
        mean_var = sb("mean_var", [P, TT, 2])
        var_eps = sb("var_eps", [P, TT])
        std = sb("std", [P, TT])
        rstd = sb("rstd", [P, TT])
        x_norm = sb("x_norm", [P, TT, D])
        h_t = sb("h_t", [P, KD, L])
        xs = sb("xs", [P, KI, L])
        silu_z = sb("silu_z", [P, KI, L])
        dt = sb("dt", [P, KI, L])
        dtx = sb("dtx", [P, KI, L])
        bc_rest = sb("bc_rest", [P, L])
        bc_parts = sb("bc_parts", [P, 3, L], BF16)
        y_gated = sb("y_gated", [P, 2, KI, L])
        scan_in = sb("scan_in", [P, 2 * RING, L])
        decay = scan_in[:, 0:RING, :]
        inflow = scan_in[:, RING:2 * RING, :]
        state = sb("state", [P, RING, L])
        c_rows = sb("c_rows", [P, 2, L])
        log_part = state
        readout = xs

        mod_w = y_gated[:, :, :, :].rearrange("p a k l -> p (a k l)").rearrange("p (k i w d) -> p k i w d", k=KD, i=4, w=2)
        gate_w = log_part[:, :, :].rearrange("p k l -> p (k l)").rearrange("p (k g d) -> p k g d", k=KD, g=4)
        gate_b = c_rows[:, :, :].rearrange("p a (g d) -> p (a g) d", d=D)

        gated = x_norm
        qk = xs[:, :, :]
        qk_sq = silu_z[:, :, :]
        v_ones = sb("v_ones", [P, TT, H, VW])
        qk_pad = scan_in[:, :, :].rearrange("p r l -> p (r l)").rearrange("p (t g c) -> p t g c", t=TT, g=2 * NG)
        norm_sq = sb("norm_sq", [P, TT, 2 * H])
        norm = sb("norm", [P, TT, 2 * H])
        norm_max = sb("norm_max", [P, TT, 2 * H])
        norm_inv = sb("norm_inv", [P, TT, 2 * H])
        q_t = dt[:, :, :]
        k_t = dtx[:, :, :]
        row_max = sb("row_max", [P, 2, TT])
        neg_max = sb("neg_max", [P, 2, TT])
        probs = y_gated[:, 0, :, :]
        probs_t = y_gated[:, 1, :, :]
        sum_inv = sb("sum_inv", [P, 2, TT])
        o_rows = state[:, 0:2, :].rearrange("p r l -> p (r l)").rearrange("p (t d) -> p t d", d=D)
        o_t = state[:, 2:2 + KD, :]
        biased = dt[:, 0:2, :].rearrange("p r l -> p (r l)").rearrange("p (t d) -> p t d", d=D)
        silu_a = log_part[:, :, :]
        ab = xs[:, :, :]
        gelu_h = y_gated[:, :, :, :].rearrange("p a k l -> p (a k) l")

        banks = [ctx.enter_context(nc.psum_tensor(f"bank{i}", [P, 512], F32)) for i in range(8)]

        first_loaded = sem("first_loaded")
        ssm_loaded = sem("ssm_loaded")
        rest_loaded = sem("rest_loaded")
        x_loaded = sem("x_loaded")
        w12_loaded = sem("w12_loaded")
        fc1_loaded = sem("fc1_loaded")
        xproj0_loaded = sem("xproj0_loaded")
        in0_loaded = sem("in0_loaded")
        out_stored = sem("out_stored")
        wait_over = sem("wait_over")
        ident_zero = sem("ident_zero")
        ident_ready = sem("ident_ready")
        ones_ready = sem("ones_ready")
        pads_ready = sem("pads_ready")
        diag_ready = sem("diag_ready")
        cond_ready = sem("cond_ready")
        a_exp_done = sem("a_exp_done")
        a_ready = sem("a_ready")
        cap_ready = sem("cap_ready")
        q_scale_ready = sem("q_scale_ready")
        mod_mm = sem("mod_mm")
        mod_sum = sem("mod_sum")
        mod_ready = sem("mod_ready")
        gate_mm = sem("gate_mm")
        gate_ready = sem("gate_ready")
        ln_stat = sem("ln_stat")
        ln_aggr = sem("ln_aggr")
        ln_var = sem("ln_var")
        ln_std = sem("ln_std")
        ln_rstd = sem("ln_rstd")
        ln_norm = sem("ln_norm")
        ln_turned = sem("ln_turned")
        ln_ready = sem("ln_ready")
        in_mm = sem("in_mm")
        in_ready = sem("in_ready")
        xproj_mm = sem("xproj_mm")
        dt_relu = sem("dt_relu")
        dt_abs = sem("dt_abs")
        dt_exp = sem("dt_exp")
        dt_log = sem("dt_log")
        dt_ready = sem("dt_ready")
        dtx_ready = sem("dtx_ready")
        bc_ready = sem("bc_ready")
        bc_spread = sem("bc_spread")
        c_copied = sem("c_copied")
        decay_ready = sem("decay_ready")
        inflow_ready = sem("inflow_ready")
        scanned = sem("scanned")
        read_out = sem("read_out")
        summed = sem("summed")
        y_ready = sem("y_ready")
        res_mm = sem("res_mm")
        res_biased = sem("res_biased")
        res_gated = sem("res_gated")
        res_ready = sem("res_ready")
        mlp_mm = sem("mlp_mm")
        mlp_silu = sem("mlp_silu")
        mlp_ready = sem("mlp_ready")
        qkv_mm = sem("qkv_mm")
        qk_ready = sem("qk_ready")
        v_ready = sem("v_ready")
        sq_ready = sem("sq_ready")
        norm_sq_ready = sem("norm_sq_ready")
        norm_ready = sem("norm_ready")
        norm_max_ready = sem("norm_max_ready")
        norm_inv_ready = sem("norm_inv_ready")
        q_inv_ready = sem("q_inv_ready")
        qk_unit = sem("qk_unit")
        qk_turned = sem("qk_turned")
        qk_t_ready = sem("qk_t_ready")
        scores_mm = sem("scores_mm")
        max_ready = sem("max_ready")
        neg_ready = sem("neg_ready")
        probs_ready = sem("probs_ready")
        probs_turned = sem("probs_turned")
        probs_t_even = sem("probs_t_even")
        probs_t_odd = sem("probs_t_odd")
        pv_mm = sem("pv_mm")
        sum_inv_ready = sem("sum_inv_ready")
        o_ready = sem("o_ready")
        o_turned = sem("o_turned")
        o_t_ready = sem("o_t_ready")
        fc1_mm = sem("fc1_mm")
        fc1_ready = sem("fc1_ready")

        FIRST = ["cond", "mod_w", "mod_b", "gate_w", "gate_b"]
        SSM = ["in_w1", "xproj_w1", "dt_b", "a_log", "d_skip", "out_w"]
        REST = ["w3", "qkv_w", "row_b", "scale_mul", "proj_w", "fc1_b", "fc2_w"]
        home = dict(cond=cond[:], mod_w=mod_w, mod_b=mod_b[:], gate_w=gate_w, gate_b=gate_b, in_w0=in_w0[:], in_w1=in_w1[:], xproj_w0=xproj_w0[:],
                    xproj_w1=xproj_w1[:],                    dt_b=dt_b[:], a_log=a_log[:], d_skip=d_skip[:], out_w=out_w[:], w12=w12, w3=w3[:], qkv_w=qkv_w[:],
                    row_b=row_b[:], scale_mul=scale_mul[:], proj_w=proj_w[:], fc1_w=fc1_w[:], fc1_b=fc1_b[:], fc2_w=fc2_w[:])
        ROWS = ("gate_b", "row_b", "scale_mul")

        def load(eng, name, signal):
            if name[-1] in "01":
                src = inp[name[:-1]][int(name[-1])]
            else:
                src = inp[name].partition_broadcast(P) if name in ROWS else inp[name]
            if name == "scale_mul":
                src = inp[name][0, :].partition_broadcast(P)
            eng.dma_start(home[name], src).then_inc(signal, 16)

        RES = 4
        x_of = [x_in, x_ssm, x_mlp, x_att, x_out]
        x_rows = inp["x"].rearrange("b (t p) d -> b p t d", p=P)
        out_rows = out.rearrange("b (t p) d -> b p t d", p=P)

        block = ctx.enter_context(nc.Block())

        @block.sync
        def _(sp):
            sp.sem_inc(out_stored, 16)
            for name in FIRST:
                load(sp, name, first_loaded)
            sp.dma_start(x_in[:], x_rows[0]).then_inc(x_loaded, 16)
            load(sp, "in_w0", in0_loaded)
            load(sp, "xproj_w0", xproj0_loaded)
            for name in SSM:
                load(sp, name, ssm_loaded)
            for name in REST:
                load(sp, name, rest_loaded)

            def turns(b, last):
                sp.wait_ge(xproj_mm, b * 2 * (KI + 1) + KI + 1)
                load(sp, "w12", w12_loaded)
                sp.dma_start(fc1_w[:], inp["fc1_w"]).then_inc(fc1_loaded, 16)
                if not last:
                    sp.wait_ge(res_ready, (b * RES + 1) * 2)
                    sp.dma_start(x_in[:], x_rows[b + 1]).then_inc(x_loaded, 16)
                    sp.wait_ge(mlp_mm, (b + 1) * 2 * KH)
                    load(sp, "xproj_w0", xproj0_loaded)
                    sp.wait_ge(fc1_mm, (b + 1) * KF)
                    load(sp, "in_w0", in0_loaded)
                sp.wait_ge(res_ready, (b * RES + RES) * 2)
                sp.dma_start(out_rows[b], x_out[:]).then_inc(out_stored, 16)

            with sp.Fori(0, B - 1) as b:
                turns(b, False)
            turns(B - 1, True)
            sp.wait_ge(out_stored, 16 * (B + 1))

        @block.gpsimd
        def _(pool):
            pool.memset(ident[:], 0.0).then_inc(ident_zero, 1)
            pool.memset(v_ones[:], 1.0).then_inc(ones_ready, 1)
            pool.wait_ge(ident_zero, 1)
            pool.affine_select(out=ident[:], in_=ident[:], compare_op=ALU.not_equal, fill=1.0, base=0,
                               pattern=[[-1, P]], channel_multiplier=1).then_inc(ident_ready, 1)
            pool.wait_ge(ident_ready, 1)
            pool.tensor_copy(ident_bf[:], ident[:]).then_inc(ident_ready, 1)
            pool.wait_ge(ssm_loaded, 16 * len(SSM))
            for d in range(2):
                for k in range(KI):
                    pool.tensor_scalar(d_diag[:, d, k, :], ident[:], d_skip[:, d, k:k + 1], None,
                                       ALU.mult).then_inc(diag_ready, 1)
            pool.sem_inc(read_out, CREDIT)
            with pool.Fori(0, B) as b:
                for d in range(2):
                    n = b * 2 + d
                    for k in range(KI):
                        pool.wait_ge(dt_ready, n * KI + k + 1)
                        pool.tensor_tensor(dtx[:, k, :], dt[:, k, :], xs[:, k, :], ALU.mult).then_inc(dtx_ready, 1)
                    pool.wait_ge(dtx_ready, (n + 1) * KI)
                    pool.sem_inc(wait_over, 1)
                    with pool.Fori(0, NS // 2) as i:
                        for j in range(2):
                            row = n * NS + i * 2 + j
                            pool.wait_ge(c_copied, row + 1 + 2)
                            for k in range(KI):
                                pool.wait_ge(scanned, row * KI + k + 1 + CREDIT)
                                pool.wait_ge(summed, (n + row) * KI + k + 1)
                                pool.tensor_tensor(readout[:, k, :], state[:, k, :], c_rows[:, j, :],
                                                   ALU.mult).then_inc(read_out, 1)
                pool.wait_ge(y_ready, (b + 1) * 2 * KI)
                pool.sem_inc(wait_over, 1)
                pool.memset(qk_pad[:], 0.0).then_inc(pads_ready, 1)
                for t in range(TT):
                    pool.wait_ge(qk_ready, b * TT + t + 1)
                    pool.tensor_tensor(qk_sq[:, t, :], qk[:, t, :], qk[:, t, :], ALU.mult).then_inc(sq_ready, 1)

        @block.scalar
        def _(act):
            act.wait_ge(first_loaded, 16 * len(FIRST))
            act.activation(silu_cond[:], cond[:], ACT.Silu).then_inc(cond_ready, 1)
            act.wait_ge(ssm_loaded, 16 * len(SSM))
            act.activation(a_exp[:], a_log[:], ACT.Exp).then_inc(a_exp_done, 1)
            act.wait_ge(cap_ready, 1)
            act.activation(q_scale[:], scale_cap[:], ACT.Exp).then_inc(q_scale_ready, 1)

            def ln(b, i):
                n = b * 4 + i
                act.wait_ge(ln_var, n + 1)
                act.activation(std[:], var_eps[:], ACT.Sqrt).then_inc(ln_std, 1)
                act.wait_ge(ln_turned, n + 1)
                act.activation(h_t[:, 1, :], banks[1][:], ACT.Identity, bias=mod[:, i, SHIFT, 1, bass.ds(b, 1)],
                               scale=mod[:, i, SCALE, 1, bass.ds(b, 1)]).then_inc(ln_ready, 1)

            act.sem_inc(c_copied, 2)
            act.wait_ge(mod_ready, 2)
            act.wait_ge(gate_ready, 4 * B)
            act.wait_ge(a_ready, 1)
            a_pairs = a_neg[:].rearrange("p d k (i j) -> p d k i j", j=2)
            with act.Fori(0, B) as b:
                ln(b, 0)
                for d in range(2):
                    n = b * 2 + d
                    for m in range(2 * KI):
                        act.wait_ge(in_mm, n * 2 * KI + m + 1)
                        to = xs[:, m, :] if m < KI else silu_z[:, m - KI, :]
                        act.activation(to, banks[m][:], ACT.Silu).then_inc(in_ready, 1)
                    for k in range(KI):
                        act.wait_ge(dt_relu, n * KI + k + 1)
                        act.activation(log_part[:, k, :], banks[k][:], ACT.Abs,
                                       bias=dt_b[:, d, k:k + 1]).then_inc(dt_abs, 1)
                    act.wait_ge(dt_abs, (n + 1) * KI)
                    act.activation(log_part[:], log_part[:], ACT.Exp, scale=-1.0).then_inc(dt_exp, 1)
                    act.wait_ge(dt_exp, n + 1)
                    act.activation(log_part[:], log_part[:], ACT.Ln, bias=1.0).then_inc(dt_log, 1)
                    act.wait_ge(dt_ready, (n + 1) * KI)
                    with act.Fori(0, NS // 2) as i:
                        for j in range(2):
                            row = n * NS + i * 2 + j
                            act.wait_ge(bc_spread, row + 1)
                            act.wait_ge(read_out, (row - 1) * KI + CREDIT)
                            act.activation(c_rows[:, j, :], banks[2 + j][:], ACT.Copy).then_inc(c_copied, 1)
                            for k in range(KI):
                                act.wait_ge(scanned, row * KI + k + 1 + CREDIT - RING)
                                act.activation(decay[:, k, :], dt[:, k, :], ACT.Exp,
                                               scale=a_pairs[:, d, k, i, j:j + 1]).then_inc(decay_ready, 1)
                ln(b, 1)
                for m in range(KH):
                    act.wait_ge(mlp_mm, (b * KH + m) * 2 + 1)
                    act.activation(silu_a[:, m, :], banks[m][:], ACT.Silu).then_inc(mlp_silu, 1)
                ln(b, 2)
                act.wait_ge(norm_sq_ready, b + 1)
                act.activation(norm[:], norm_sq[:], ACT.Sqrt).then_inc(norm_ready, 1)
                for i in range(0, 2 * NG, 2):
                    act.wait_ge(qk_turned, b * 2 * NG + i + 1)
                    to = q_t[:, i, :] if i < NG else k_t[:, i - NG, :]
                    act.activation(to, banks[i][:], ACT.Copy).then_inc(qk_t_ready, 1)
                for h in range(H):
                    n = b * H + h
                    act.wait_ge(neg_ready, n + 1)
                    for t in range(TT):
                        act.activation(probs[:, t, :], banks[t][:], ACT.Exp,
                                       bias=neg_max[:, h % 2, t:t + 1]).then_inc(probs_ready, 1)
                    for kt in range(0, TT, 2):
                        act.wait_ge(probs_turned, n * TT + kt + 1)
                        act.activation(probs_t[:, kt, :], banks[4 + kt % 3][:], ACT.Copy).then_inc(probs_t_even, 1)
                act.wait_ge(o_turned, b + 1)
                act.activation(o_t[:, 1, :], banks[1][:], ACT.Copy).then_inc(o_t_ready, 1)
                ln(b, 3)
                for m in range(KF):
                    act.wait_ge(fc1_mm, b * KF + m + 1)
                    act.activation(gelu_h[:, m, :], banks[m][:], ACT.Gelu, bias=fc1_b[:, m:m + 1]).then_inc(fc1_ready, 1)

        @block.tensor
        def _(pe):
            pe.wait_ge(ident_ready, 2)
            pe.wait_ge(first_loaded, 16 * len(FIRST))
            pe.wait_ge(cond_ready, 1)
            for i in range(4):
                c = cond if i < 2 else silu_cond
                for w in range(2):
                    for f in range(KD):
                        at = ((i * 2 + w) * KD + f) * B
                        for kc in range(KD):
                            last = pe.matmul(banks[0][:, at:at + B], mod_w[:, kc, i, w, f * P:(f + 1) * P], c[:, kc, :],
                                             start=(kc == 0), stop=(kc == KD - 1))
            last.then_inc(mod_mm, 1)
            for b in range(B):
                for g in range(4):
                    c = cond if g < 2 else silu_cond
                    u = b * 4 + g
                    if u >= 4:
                        pe.wait_ge(gate_ready, u - 3)
                    for kc in range(KD):
                        last = pe.matmul(banks[1 + u % 4][:, 0:D], c[:, kc, b:b + 1].to_broadcast([P, P]),
                                         gate_w[:, kc, g, :], start=(kc == 0), stop=(kc == KD - 1))
                    last.then_inc(gate_mm, 1)
            pe.wait_ge(gate_ready, 4 * B)
            pe.wait_ge(mod_ready, 2)
            pe.wait_ge(ssm_loaded, 16 * len(SSM))
            pe.wait_ge(diag_ready, 2 * KI)
            def ln(b, i):
                n = b * 4 + i
                for t in range(TT):
                    pe.wait_ge(ln_norm, n * TT + t + 1)
                    for f in range(KD):
                        last = pe.transpose(banks[f][:, t * P:(t + 1) * P], x_norm[:, t, f * P:(f + 1) * P], ident[:])
                last.then_inc(ln_turned, 1)
                pe.wait_ge(ln_ready, (n + 1) * KD)

            ident_pairs = ident_bf[:].rearrange("p (i j) -> p i j", j=2)

            def spread(n, i, j):
                row = n * NS + i * 2 + j
                pe.wait_ge(inflow_ready, (row - 1) * KI + CREDIT)
                pe.wait_ge(c_copied, row + 1)
                for to, half in ((j, 0), (2 + j, NS // 2)):
                    for part in range(3):
                        last = pe.matmul(banks[to][:], ident_pairs[:, i + half, j:j + 1].to_broadcast([P, P]),
                                         bc_parts[:, part, :], start=(part == 0), stop=(part == 2))
                last.then_inc(bc_spread, 1)

            def sums(n, s):
                row = n * NS + s
                for k in range(KI):
                    pe.wait_ge(read_out, row * KI + k + 1 + CREDIT)
                    pe.matmul(banks[4 + k][:], ident[:], readout[:, k, :], start=False, stop=True,
                              skip_group_check=True).then_inc(summed, 1)

            def residual_rows(lhs, rhs, steps):
                for t in range(TT):
                    for c in range(steps):
                        last = pe.matmul(banks[t // 2][:, (t % 2) * D:(t % 2 + 1) * D], lhs(c, t), rhs(c),
                                         start=(c == 0), stop=(c == steps - 1))
                    if t % 2:
                        last.then_inc(res_mm, 1)

            with pe.Fori(0, B) as b:
                ln(b, 0)
                for d in range(2):
                    n = b * 2 + d
                    if d == 1:
                        pe.wait_ge(y_ready, n * KI)
                    else:
                        pe.wait_ge(in0_loaded, 16 * (b + 1))
                        pe.wait_ge(xproj0_loaded, 16 * (b + 1))
                    for m in range(2 * KI):
                        for kc in range(KD):
                            last = pe.matmul(banks[m][:], in_w[d][:, kc, m * P:(m + 1) * P], h_t[:, kc, :],
                                             start=(kc == 0), stop=(kc == KD - 1))
                        last.then_inc(in_mm, 1)
                    pe.wait_ge(in_ready, (n + 1) * 2 * KI)
                    for m in range(KI + 1):
                        for kc in range(KI):
                            last = pe.matmul(banks[m][:], xproj_w[d][:, kc, m * P:(m + 1) * P], xs[:, kc, :],
                                             start=(kc == 0), stop=(kc == KI - 1))
                        last.then_inc(xproj_mm, 1)
                    pe.wait_ge(bc_ready, (n + 1) * 5)
                    pe.wait_ge(dt_abs, (n + 1) * KI)
                    pe.wait_ge(dt_relu, (n + 1) * KI)
                    for k in range(KI):
                        pe.matmul(banks[4 + k][:], d_diag[:, d, k, :], xs[:, k, :], start=True,
                                  stop=True).then_inc(summed, 1)
                    spread(n, 0, 0)
                    with pe.Fori(0, NS // 2 - 1) as i:
                        spread(n, i, 1)
                        sums(n, i * 2)
                        spread(n, i + 1, 0)
                        sums(n, i * 2 + 1)
                    spread(n, NS // 2 - 1, 1)
                    sums(n, NS - 2)
                    sums(n, NS - 1)
                pe.wait_ge(y_ready, (b + 1) * 2 * KI)
                residual_rows(lambda c, t: y_gated[:, c // KI, c % KI, t * P:(t + 1) * P],
                              lambda c: out_w[:, c // KI, c % KI, :], 2 * KI)
                ln(b, 1)
                pe.wait_ge(rest_loaded, 16 * len(REST))
                pe.wait_ge(w12_loaded, 16 * (b + 1))
                for m in range(KH):
                    for w in range(2):
                        for kc in range(KD):
                            last = pe.matmul(banks[m + w * KH][:], w12[:, w, kc, m * P:(m + 1) * P], h_t[:, kc, :],
                                             start=(kc == 0), stop=(kc == KD - 1))
                        last.then_inc(mlp_mm, 1)
                pe.wait_ge(mlp_ready, (b + 1) * KH)
                residual_rows(lambda c, t: ab[:, c, t * P:(t + 1) * P], lambda c: w3[:, c, :], KH)
                ln(b, 2)
                for t in range(TT):
                    for kc in range(KD):
                        pe.matmul(banks[t][:], h_t[:, kc, t * P:(t + 1) * P], qkv_w[:, kc, 0:2 * D],
                                  start=(kc == 0), stop=(kc == KD - 1))
                    for kc in range(KD):
                        last = pe.matmul(banks[4 + t][:, 0:D], h_t[:, kc, t * P:(t + 1) * P], qkv_w[:, kc, 2 * D:3 * D],
                                         start=(kc == 0), stop=(kc == KD - 1))
                    last.then_inc(qkv_mm, 1)
                pe.wait_ge(v_ready, (b + 1) * TT)
                for i in range(2 * NG):
                    for t in range(TT):
                        pe.wait_ge(qk_unit, b * TT + t + 1)
                        last = pe.transpose(banks[i][:, t * P:(t + 1) * P], qk_pad[:, t, i, :], ident[:])
                    last.then_inc(qk_turned, 1)
                pe.wait_ge(qk_t_ready, (b + 1) * 2 * NG)

                def scores(h):
                    a, g = (h % HG) * LANE, h // HG
                    if h:
                        pe.wait_ge(probs_ready, (b * H + h) * TT)
                    for t in range(TT):
                        last = pe.matmul(banks[t][:], q_t[a:a + HD, g, t * P:(t + 1) * P], k_t[a:a + HD, g, :],
                                         start=True, stop=True)
                    last.then_inc(scores_mm, 1)

                def turn(h):
                    pe.wait_ge(probs_ready, (b * H + h + 1) * TT)
                    for kt in range(TT):
                        if kt == 3:
                            pe.wait_ge(probs_t_even, (b * H + h) * 2 + 1)
                        for t in range(TT):
                            last = pe.transpose(banks[4 + kt % 3][:, t * P:(t + 1) * P],
                                                probs[:, t, kt * P:(kt + 1) * P], ident[:])
                        last.then_inc(probs_turned, 1)

                def weigh(h):
                    n = b * H + h
                    at = (h % 2) * TT * VW
                    pe.wait_ge(probs_t_even, (n + 1) * 2)
                    pe.wait_ge(probs_t_odd, (n + 1) * 2)
                    if h:
                        pe.wait_ge(o_ready, n)
                    for t in range(TT):
                        for kt in range(TT):
                            last = pe.matmul(banks[7][:, at + t * VW:at + (t + 1) * VW],
                                             probs_t[:, kt, t * P:(t + 1) * P], v_ones[:, kt, h, :],
                                             start=(kt == 0), stop=(kt == TT - 1))
                    last.then_inc(pv_mm, 1)

                scores(0)
                for h in range(H):
                    turn(h)
                    if h + 1 < H:
                        scores(h + 1)
                    weigh(h)
                pe.wait_ge(o_ready, (b + 1) * H)
                for t in range(TT):
                    for f in range(KD):
                        last = pe.transpose(banks[f][:, t * P:(t + 1) * P], o_rows[:, t, f * P:(f + 1) * P], ident[:])
                last.then_inc(o_turned, 1)
                pe.wait_ge(o_t_ready, (b + 1) * KD)
                residual_rows(lambda c, t: o_t[:, c, t * P:(t + 1) * P], lambda c: proj_w[:, c, :], KD)
                ln(b, 3)
                pe.wait_ge(fc1_loaded, 16 * (b + 1))
                for m in range(KF):
                    for kc in range(KD):
                        last = pe.matmul(banks[m][:], fc1_w[:, kc, m * P:(m + 1) * P], h_t[:, kc, :],
                                         start=(kc == 0), stop=(kc == KD - 1))
                    last.then_inc(fc1_mm, 1)
                pe.wait_ge(fc1_ready, (b + 1) * KF)
                residual_rows(lambda c, t: gelu_h[:, c, t * P:(t + 1) * P], lambda c: fc2_w[:, c, :], KF)

        @block.vector
        def _(dve):
            dve.wait_ge(first_loaded, 16 * len(FIRST))
            dve.wait_ge(mod_mm, 1)
            dve.tensor_tensor(mod[:].rearrange("p i w f b -> p (i w f) b"),
                              banks[0][:, 0:16 * B].rearrange("p (g b) -> p g b", b=B),
                              mod_b[:].rearrange("p i w f -> p (i w f)").unsqueeze(2).to_broadcast([P, 16, B]),
                              ALU.add).then_inc(mod_sum, 1)
            dve.wait_ge(mod_sum, 1)
            one_plus = mod[:, :, SCALE, :, :].rearrange("p i f b -> p i (f b)")
            dve.tensor_scalar(one_plus, one_plus, 1.0, None, ALU.add).then_inc(mod_ready, 2)
            for b in range(B):
                for g in range(4):
                    u = b * 4 + g
                    dve.wait_ge(gate_mm, u + 1)
                    dve.tensor_tensor(gate[:, b, g, :], banks[1 + u % 4][:, 0:D], gate_b[:, g, :],
                                      ALU.add).then_inc(gate_ready, 1)
            dve.wait_ge(a_exp_done, 1)
            dve.tensor_scalar(a_neg[:], a_exp[:], -1.0, None, ALU.mult).then_inc(a_ready, 1)
            dve.wait_ge(rest_loaded, 16 * len(REST))
            dve.tensor_scalar(scale_cap[:], scale_mul[:], MAX_SCALE_MUL, None, ALU.min).then_inc(cap_ready, 1)
            dve.wait_ge(gate_ready, 4 * B)
            dve.wait_ge(mod_ready, 2)
            dve.wait_ge(ones_ready, 1)
            dve.wait_ge(q_scale_ready, 1)
            dve.sem_inc(inflow_ready, CREDIT)
            dve.sem_inc(scanned, CREDIT)

            def ln(b, i, x, eps):
                n = b * 4 + i
                if i:
                    dve.wait_ge(res_ready, (b * RES + i) * 2)
                for t in range(TT):
                    dve.bn_stats(stats[:, t, :], x[:, t, :]).then_inc(ln_stat, 1)
                dve.wait_ge(ln_stat, (n + 1) * TT)
                dve.sem_inc(wait_over, 1)
                for t in range(TT):
                    dve.bn_aggr(mean_var[:, t, :], stats[:, t, :]).then_inc(ln_aggr, 1)
                dve.wait_ge(ln_aggr, (n + 1) * TT)
                dve.tensor_scalar(var_eps[:], mean_var[:, :, 1], eps, None, ALU.add).then_inc(ln_var, 1)
                dve.wait_ge(ln_std, n + 1)
                dve.reciprocal(rstd[:], std[:]).then_inc(ln_rstd, 1)
                dve.wait_ge(ln_rstd, n + 1)
                for t in range(TT):
                    dve.tensor_scalar(x_norm[:, t, :], x[:, t, :], mean_var[:, t, 0:1], rstd[:, t:t + 1],
                                      ALU.subtract, ALU.mult).then_inc(ln_norm, 1)
                dve.wait_ge(ln_turned, n + 1)
                dve.tensor_scalar(h_t[:, 0, :], banks[0][:], mod[:, i, SCALE, 0, bass.ds(b, 1)], mod[:, i, SHIFT, 0, bass.ds(b, 1)],
                                  ALU.mult, ALU.add).then_inc(ln_ready, 1)

            def residual(b, i, g, bias=None):
                for p in range(2):
                    n = (b * RES + i) * 2 + p
                    tiles = slice(2 * p, 2 * p + 2)
                    dve.wait_ge(res_mm, n + 1)
                    src = banks[p][:].rearrange("p (t d) -> p t d", d=D)
                    if bias is not None:
                        dve.tensor_tensor(biased[:, tiles, :], src, row_b[:, bias:bias + 1, :].to_broadcast([P, 2, D]),
                                          ALU.add).then_inc(res_biased, 1)
                        dve.wait_ge(res_biased, b * 4 + (2 if i == 3 else 0) + p + 1)
                        src = biased[:, tiles, :]
                    dve.tensor_tensor(gated[:, tiles, :], src, gate[:, b, g, :].unsqueeze(1).to_broadcast([P, 2, D]),
                                      ALU.mult).then_inc(res_gated, 1)
                    dve.wait_ge(res_gated, n + 1)
                    dve.tensor_tensor(x_of[i + 1][:, tiles, :], x_of[i][:, tiles, :], gated[:, tiles, :],
                                      ALU.add).then_inc(res_ready, 1)

            with dve.Fori(0, B) as b:
                dve.wait_ge(x_loaded, (b + 1) * 16)
                ln(b, 0, x_in, EPS_MAMBA)
                for d in range(2):
                    n = b * 2 + d
                    for k in range(KI):
                        dve.wait_ge(xproj_mm, n * (KI + 1) + k + 1)
                        dve.tensor_scalar(dt[:, k, :], banks[k][:], dt_b[:, d, k:k + 1], 0.0,
                                          ALU.add, ALU.max).then_inc(dt_relu, 1)
                    dve.wait_ge(xproj_mm, (n + 1) * (KI + 1))
                    dve.tensor_copy(bc_parts[:, 0, :], banks[KI][:]).then_inc(bc_ready, 1)
                    dve.wait_ge(bc_ready, n * 5 + 1)
                    dve.tensor_tensor(bc_rest[:], banks[KI][:], bc_parts[:, 0, :], ALU.subtract).then_inc(bc_ready, 1)
                    dve.wait_ge(bc_ready, n * 5 + 2)
                    dve.tensor_copy(bc_parts[:, 1, :], bc_rest[:]).then_inc(bc_ready, 1)
                    dve.wait_ge(bc_ready, n * 5 + 3)
                    dve.tensor_tensor(bc_rest[:], bc_rest[:], bc_parts[:, 1, :], ALU.subtract).then_inc(bc_ready, 1)
                    dve.wait_ge(bc_ready, n * 5 + 4)
                    dve.tensor_copy(bc_parts[:, 2, :], bc_rest[:]).then_inc(bc_ready, 1)
                    dve.wait_ge(dt_log, n + 1)
                    dve.wait_ge(dt_relu, (n + 1) * KI)
                    for k in range(KI):
                        dve.tensor_tensor(dt[:, k, :], dt[:, k, :], log_part[:, k, :], ALU.add).then_inc(dt_ready, 1)
                    dve.wait_ge(dtx_ready, (n + 1) * KI)
                    dve.sem_inc(wait_over, 1)
                    time = slice(None, None, -1) if d else slice(None)

                    def inflow_of(row, j, k):
                        dve.tensor_tensor(inflow[:, k, :], dtx[:, k, :], banks[j][:], ALU.mult).then_inc(inflow_ready, 1)

                    def scan(row, k):
                        unit = row * KI + k
                        dve.wait_ge(decay_ready, unit + 1)
                        dve.wait_ge(inflow_ready, unit + 1 + CREDIT)
                        dve.wait_ge(read_out, unit + 1 + CREDIT - RING)
                        dve.tensor_tensor_scan(state[:, k, time], decay[:, k, time], inflow[:, k, time], 0.0,
                                               ALU.mult, ALU.add).then_inc(scanned, 1)

                    with dve.Fori(0, NS // 2) as i:
                        for j in range(2):
                            row = n * NS + i * 2 + j
                            dve.wait_ge(bc_spread, row + 1)
                            for k in range(KI):
                                dve.wait_ge(scanned, row * KI + k + 1 + CREDIT - RING)
                                inflow_of(row, j, k)
                                if k:
                                    scan(row, k - 1)
                            scan(row, KI - 1)
                    for k in range(KI):
                        dve.wait_ge(summed, ((n + 1) * (NS + 1) - 1) * KI + k + 1)
                        dve.tensor_tensor(y_gated[:, d, k, :], banks[4 + k][:], silu_z[:, k, :],
                                          ALU.mult).then_inc(y_ready, 1)
                residual(b, 0, GATE_MAMBA)
                ln(b, 1, x_ssm, EPS_MAMBA)
                dve.wait_ge(out_stored, 16 * (b + 1))
                for m in range(KH):
                    dve.wait_ge(mlp_silu, b * KH + m + 1)
                    dve.wait_ge(mlp_mm, (b * KH + m + 1) * 2)
                    dve.tensor_tensor(ab[:, m, :], banks[4 + m][:], silu_a[:, m, :], ALU.mult).then_inc(mlp_ready, 1)
                residual(b, 1, GATE_MLP)
                ln(b, 2, x_mlp, EPS_LN)
                for t in range(TT):
                    dve.wait_ge(qkv_mm, b * TT + t + 1)
                    dve.tensor_tensor(qk[:, t, 0:D], banks[t][:, 0:D], row_b[:, Q_BIAS, :], ALU.add)
                    dve.tensor_copy(qk[:, t, D:2 * D], banks[t][:, D:2 * D]).then_inc(qk_ready, 1)
                    dve.tensor_tensor(v_ones[:, t, :, 0:HD], banks[4 + t][:, 0:D].rearrange("p (h e) -> p h e", e=HD),
                                      row_b[:, V_BIAS, :].rearrange("p (h e) -> p h e", e=HD),
                                      ALU.add).then_inc(v_ready, 1)
                dve.wait_ge(sq_ready, (b + 1) * TT)
                dve.tensor_reduce(norm_sq[:], qk_sq.rearrange("p t (h e) -> p t h e", e=HD), AX.X,
                                  ALU.add).then_inc(norm_sq_ready, 1)
                dve.wait_ge(norm_ready, b + 1)
                dve.tensor_scalar(norm_max[:], norm[:], EPS_NORM, None, ALU.max).then_inc(norm_max_ready, 1)
                dve.wait_ge(norm_max_ready, b + 1)
                dve.reciprocal(norm_inv[:], norm_max[:]).then_inc(norm_inv_ready, 1)
                dve.wait_ge(norm_inv_ready, b + 1)
                dve.tensor_tensor(norm_inv[:, :, 0:H], norm_inv[:, :, 0:H],
                                  q_scale[:].unsqueeze(1).to_broadcast([P, TT, H]), ALU.mult).then_inc(q_inv_ready, 1)
                dve.wait_ge(q_inv_ready, b + 1)
                dve.wait_ge(pads_ready, b + 1)
                for t in range(TT):
                    pad = qk_pad[:, t, :, :].rearrange("p g (h e) -> p (g h) e", e=LANE)
                    dve.tensor_tensor(pad[:, :, 0:HD], qk[:, t, :].rearrange("p (h e) -> p h e", e=HD),
                                      norm_inv[:, t, :].unsqueeze(2).to_broadcast([P, 2 * H, HD]),
                                      ALU.mult).then_inc(qk_unit, 1)
                for i in range(1, 2 * NG, 2):
                    dve.wait_ge(qk_turned, b * 2 * NG + i + 1)
                    to = q_t[:, i, :] if i < NG else k_t[:, i - NG, :]
                    dve.tensor_copy(to, banks[i][:]).then_inc(qk_t_ready, 1)

                def maxima(h):
                    n = b * H + h
                    dve.wait_ge(scores_mm, n + 1)
                    for t in range(TT):
                        last = dve.tensor_reduce(row_max[:, h % 2, t:t + 1], banks[t][:], AX.X, ALU.max)
                    last.then_inc(max_ready, 1)
                    dve.wait_ge(max_ready, n + 1)
                    dve.tensor_scalar(neg_max[:, h % 2, :], row_max[:, h % 2, :], -1.0, None, ALU.mult).then_inc(neg_ready, 1)

                def divide(h):
                    n = b * H + h
                    o = banks[7][:, (h % 2) * TT * VW:(h % 2 + 1) * TT * VW].rearrange("p (t e) -> p t e", e=VW)
                    dve.wait_ge(pv_mm, n + 1)
                    dve.reciprocal(sum_inv[:, h % 2, :], o[:, :, HD]).then_inc(sum_inv_ready, 1)
                    dve.wait_ge(sum_inv_ready, n + 1)
                    dve.tensor_tensor(o_rows[:, :, h * HD:(h + 1) * HD], o[:, :, 0:HD],
                                      sum_inv[:, h % 2, :].unsqueeze(2).to_broadcast([P, TT, HD]),
                                      ALU.mult).then_inc(o_ready, 1)

                maxima(0)
                for h in range(H):
                    for kt in range(1, TT, 2):
                        dve.wait_ge(probs_turned, (b * H + h) * TT + kt + 1)
                        dve.tensor_copy(probs_t[:, kt, :], banks[4 + kt % 3][:]).then_inc(probs_t_odd, 1)
                    if h + 1 < H:
                        maxima(h + 1)
                    divide(h)
                dve.wait_ge(o_turned, b + 1)
                dve.tensor_copy(o_t[:, 0, :], banks[0][:]).then_inc(o_t_ready, 1)
                residual(b, 2, GAMMA1, PROJ_B)
                ln(b, 3, x_att, EPS_LN)
                residual(b, 3, GAMMA2, FC2_B)


def kernel(**inputs):
    import numpy as np
    import concourse.bacc as bacc
    from concourse.bass_utils import run_bass_kernel_spmd

    a = {k: np.asarray(v) for k, v in inputs.items()}

    def cut(w):
        return w.reshape(-1, P, *w.shape[1:]).swapaxes(0, 1)

    mamba_w, mlp_w, ada_w = a["L0_cond_adaln_mamba_w"], a["L0_cond_adaln_mlp_w"], a["L1_cond_ada_w"].T
    mamba_b, mlp_b, ada_b = a["L0_cond_adaln_mamba_b"], a["L0_cond_adaln_mlp_b"], a["L1_cond_ada_b"]

    def col(w, i):
        return w[..., i * D:(i + 1) * D]

    pairs_w = [(col(mamba_w, 0), col(mamba_w, 1)), (col(mlp_w, 0), col(mlp_w, 1)),
               (col(ada_w, 4), col(ada_w, 2)), (col(ada_w, 5), col(ada_w, 3))]
    pairs_b = [(col(mamba_b, 0), col(mamba_b, 1)), (col(mlp_b, 0), col(mlp_b, 1)),
               (col(ada_b, 4), col(ada_b, 2)), (col(ada_b, 5), col(ada_b, 3))]
    gates_w = [col(mamba_w, 2), col(mlp_w, 2), col(ada_w, 0), col(ada_w, 1)]
    gates_b = [col(mamba_b, 2), col(mlp_b, 2), col(ada_b, 0), col(ada_b, 1)]

    def both(name):
        return np.stack([cut(a[f"L0_cond_{d}_{name}"]) for d in ("fwd", "bwd")], 1)

    laid = {
        "x": a["x"],
        "cond": cut(a["cond_1024"].T),
        "mod_w": cut(np.stack([np.stack(p, 1) for p in pairs_w], 1)),
        "mod_b": np.stack([np.stack([v.reshape(KD, P).T for v in p], 1) for p in pairs_b], 1),
        "gate_w": cut(np.stack(gates_w, 1)),
        "gate_b": np.stack(gates_b, 0),
        "in_w": both("in_w").swapaxes(0, 1),
        "xproj_w": both("xproj_w").swapaxes(0, 1),
        "dt_b": both("dt_bias"),
        "a_log": both("A_log"),
        "d_skip": both("D"),
        "out_w": both("out_w"),
        "w12": np.stack([cut(a["L0_cond_mlp_w1"]), cut(a["L0_cond_mlp_w2"])], 1),
        "w3": cut(a["L0_cond_mlp_w3"]),
        "qkv_w": cut(a["L1_cond_mat_qkv_w"].T),
        "row_b": np.stack([a[f"L1_cond_{v}"] for v in ("q_bias", "v_bias", "proj_b", "fc2_b")], 0),
        "scale_mul": a["L1_cond_scale_mul"].reshape(1, H),
        "proj_w": cut(a["L1_cond_proj_w"].T),
        "fc1_w": cut(a["L1_cond_fc1_w"].T),
        "fc1_b": cut(a["L1_cond_fc1_b"]),
        "fc2_w": cut(a["L1_cond_fc2_w"].T),
    }
    nc = bacc.Bacc("TRN2", target_bir_lowering=False, num_devices=1)
    arrays, aps = {}, {}
    for name, shape in INPUTS.items():
        arrays[f"in_{name}"] = np.ascontiguousarray(laid[name]).reshape(shape)
        aps[name] = nc.dram_tensor(f"in_{name}", shape, F32, kind="ExternalInput").ap()
    out = nc.dram_tensor("out", [B, L, D], F32, kind="ExternalOutput").ap()
    build(nc, aps, out)
    r = run_bass_kernel_spmd(nc, [arrays], core_ids=[0])
    return r.results[0]["out"]
```

```python
from contextlib import ExitStack

import concourse.bass as bass
from concourse import mybir

F32 = mybir.dt.float32
BF16 = mybir.dt.bfloat16
ALU = mybir.AluOpType
ACT = mybir.ActivationFunctionType
AX = mybir.AxisListType

P = 128
B = 4
L = 512
D = 256
DI = 512
NS = 64
HID = 512
FF = 1024
H = 16
HD = D // H
TT = L // P
KD = D // P
KI = DI // P
KH = HID // P
KF = FF // P
LANE = 32
HG = P // LANE
NG = H // HG
STEPS = TT * NG
VW = HD + 1
PARTS = 3
QUAD = 32
RING = 4
CREDIT = RING + 1
EPS_MAMBA = 1e-5
EPS_LN = 1e-6
EPS_NORM = 1e-12
MAX_SCALE_MUL = 4.605170185988092
SHIFT, SCALE = 0, 1
GATE_MAMBA, GATE_MLP, GAMMA1, GAMMA2 = range(4)
Q_BIAS, V_BIAS, PROJ_B, FC2_B = range(4)

INPUTS = {
    "x": [B, L, D],
    "cond": [P, KD, B],
    "mod_w": [P, KD, 4, 2, D],
    "mod_b": [P, 4, 2, KD],
    "gate_w": [P, KD, 4, D],
    "gate_b": [4, D],
    "in_w": [2, P, KD, 2 * DI],
    "xproj_w": [2, P, KI, DI + 2 * NS],
    "dt_b": [P, 2, KI],
    "a_log": [P, 2, KI, NS],
    "d_skip": [P, 2, KI],
    "out_w": [P, 2, KI, D],
    "w12": [P, 2, KD, HID],
    "w3": [P, KH, D],
    "qkv_w": [P, KD, 3 * D],
    "row_b": [4, D],
    "scale_mul": [1, H],
    "proj_w": [P, KD, D],
    "fc1_w": [P, KD, FF],
    "fc1_b": [P, KF],
    "fc2_w": [P, KF, D],
}


def build(nc, inp, out):
    ctx = ExitStack()
    with ctx:
        def sb(name, shape, dtype=F32):
            return ctx.enter_context(nc.sbuf_tensor(name, shape, dtype))

        def sem(name):
            return ctx.enter_context(nc.semaphore(name))

        ident = sb("ident", [P, P])
        row_pick = sb("row_pick", [PARTS * QUAD, QUAD], BF16)
        cond = sb("cond", [P, KD, B])
        silu_cond = sb("silu_cond", [P, KD, B])
        mod_b = sb("mod_b", [P, 4, 2, KD])
        mod = sb("mod", [P, 4, 2, KD, B])
        gate = sb("gate", [P, B, 4, D])
        in_w0 = sb("in_w0", [P, KD, 2 * DI])
        in_w1 = sb("in_w1", [P, KD, 2 * DI])
        in_w = [in_w0, in_w1]
        fc1_w = in_w0
        xproj_w0 = sb("xproj_w0", [P, KI, DI + 2 * NS])
        xproj_w1 = sb("xproj_w1", [P, KI, DI + 2 * NS])
        xproj_w = [xproj_w0, xproj_w1]
        w12 = xproj_w0[:].rearrange("p k n -> p (k n)")[:, 0:2 * KD * HID].rearrange("p (w k n) -> p w k n", w=2, k=KD)
        dt_b = sb("dt_b", [P, 2, KI])
        a_log = sb("a_log", [P, 2, KI, NS])
        a_exp = sb("a_exp", [P, 2, KI, NS])
        a_neg = sb("a_neg", [P, 2, KI, NS])
        d_skip = sb("d_skip", [P, 2, KI])
        d_diag = sb("d_diag", [P, 2, KI, P])
        out_w = sb("out_w", [P, 2, KI, D])
        w3 = sb("w3", [P, KH, D])
        qkv_w = sb("qkv_w", [P, KD, 3 * D])
        row_b = sb("row_b", [P, 4, D])
        scale_mul = sb("scale_mul", [P, H])
        scale_cap = sb("scale_cap", [P, H])
        q_scale = sb("q_scale", [P, H])
        proj_w = sb("proj_w", [P, KD, D])
        fc1_b = sb("fc1_b", [P, KF])
        fc2_w = sb("fc2_w", [P, KF, D])

        x_in = sb("x_in", [P, TT, D])
        x_ssm = sb("x_ssm", [P, TT, D])
        x_mlp = sb("x_mlp", [P, TT, D])
        x_att = x_ssm
        x_out = x_mlp
        stats = sb("stats", [P, TT, 6])
        mean_var = sb("mean_var", [P, TT, 2])
        var_eps = sb("var_eps", [P, TT])
        std = sb("std", [P, TT])
        rstd = sb("rstd", [P, TT])
        x_norm = sb("x_norm", [P, TT, D])
        h_t = sb("h_t", [P, KD, L])
        xs = sb("xs", [P, KI, L])
        silu_z = sb("silu_z", [P, KI, L])
        dt = sb("dt", [P, KI, L])
        dtx = sb("dtx", [P, KI, L])
        bc_rest = sb("bc_rest", [P, L])
        bc_parts = sb("bc_parts", [P, PARTS, L], BF16)
        bc_stack = sb("bc_stack", [PARTS * QUAD, P // QUAD, L], BF16)
        y_gated = sb("y_gated", [P, 2, KI, L])
        scan_in = sb("scan_in", [P, 2 * RING, L])
        decay = scan_in[:, 0:RING, :]
        inflow = scan_in[:, RING:2 * RING, :]
        state = sb("state", [P, RING, L])
        c_rows = sb("c_rows", [P, 2, L])
        log_part = state
        readout = xs

        mod_w = y_gated[:, :, :, :].rearrange("p a k l -> p (a k l)").rearrange("p (k i w d) -> p k i w d", k=KD, i=4, w=2)
        gate_w = log_part[:, :, :].rearrange("p k l -> p (k l)").rearrange("p (k g d) -> p k g d", k=KD, g=4)
        gate_b = c_rows[:, :, :].rearrange("p a (g d) -> p (a g) d", d=D)

        gated = x_norm
        qk = xs[:, :, :]
        qk_sq = silu_z[:, :, :]
        v_ones = sb("v_ones", [P, TT, H, VW])
        qk_pad = scan_in[:, :, :].rearrange("p r l -> p (r l)").rearrange("p (t g c) -> p t g c", t=TT, g=2 * NG)
        norm_sq = sb("norm_sq", [P, TT, 2 * H])
        norm = sb("norm", [P, TT, 2 * H])
        norm_max = sb("norm_max", [P, TT, 2 * H])
        norm_inv = sb("norm_inv", [P, TT, 2 * H])
        q_t = dt[:, :, :]
        k_t = dtx[:, :, :]
        row_max = sb("row_max", [P, 2, HG])
        neg_max = sb("neg_max", [P, 2, HG])
        probs = y_gated[:, 0, :, :]
        probs_t = y_gated[:, 1, :, :]
        sum_inv = sb("sum_inv", [P, 2, HG])
        o_rows = state[:, 0:2, :].rearrange("p r l -> p (r l)").rearrange("p (t d) -> p t d", d=D)
        o_t = state[:, 2:2 + KD, :]
        biased = dt[:, 0:2, :].rearrange("p r l -> p (r l)").rearrange("p (t d) -> p t d", d=D)
        silu_a = log_part[:, :, :]
        ab = xs[:, :, :]
        gelu_h = y_gated[:, :, :, :].rearrange("p a k l -> p (a k) l")

        banks = [ctx.enter_context(nc.psum_tensor(f"bank{i}", [P, 512], F32)) for i in range(8)]

        first_loaded = sem("first_loaded")
        ssm_loaded = sem("ssm_loaded")
        rest_loaded = sem("rest_loaded")
        x_loaded = sem("x_loaded")
        w12_loaded = sem("w12_loaded")
        fc1_loaded = sem("fc1_loaded")
        xproj0_loaded = sem("xproj0_loaded")
        in0_loaded = sem("in0_loaded")
        out_stored = sem("out_stored")
        wait_over = sem("wait_over")
        ident_zero = sem("ident_zero")
        ident_ready = sem("ident_ready")
        ones_ready = sem("ones_ready")
        pads_ready = sem("pads_ready")
        diag_ready = sem("diag_ready")
        cond_ready = sem("cond_ready")
        a_exp_done = sem("a_exp_done")
        a_ready = sem("a_ready")
        cap_ready = sem("cap_ready")
        q_scale_ready = sem("q_scale_ready")
        mod_mm = sem("mod_mm")
        mod_sum = sem("mod_sum")
        mod_ready = sem("mod_ready")
        gate_mm = sem("gate_mm")
        gate_ready = sem("gate_ready")
        ln_stat = sem("ln_stat")
        ln_aggr = sem("ln_aggr")
        ln_var = sem("ln_var")
        ln_std = sem("ln_std")
        ln_rstd = sem("ln_rstd")
        ln_norm = sem("ln_norm")
        ln_turned = sem("ln_turned")
        ln_ready = sem("ln_ready")
        in_mm = sem("in_mm")
        in_ready = sem("in_ready")
        xproj_mm = sem("xproj_mm")
        dt_relu = sem("dt_relu")
        dt_abs = sem("dt_abs")
        dt_exp = sem("dt_exp")
        dt_log = sem("dt_log")
        dt_ready = sem("dt_ready")
        dtx_ready = sem("dtx_ready")
        bc_ready = sem("bc_ready")
        bc_stacked = sem("bc_stacked")
        bc_spread = sem("bc_spread")
        c_copied = sem("c_copied")
        decay_ready = sem("decay_ready")
        inflow_ready = sem("inflow_ready")
        scanned = sem("scanned")
        read_out = sem("read_out")
        summed = sem("summed")
        y_ready = sem("y_ready")
        res_mm = sem("res_mm")
        res_biased = sem("res_biased")
        res_gated = sem("res_gated")
        res_ready = sem("res_ready")
        mlp_mm = sem("mlp_mm")
        mlp_silu = sem("mlp_silu")
        mlp_ready = sem("mlp_ready")
        qkv_mm = sem("qkv_mm")
        qk_ready = sem("qk_ready")
        v_ready = sem("v_ready")
        sq_ready = sem("sq_ready")
        norm_sq_ready = sem("norm_sq_ready")
        norm_ready = sem("norm_ready")
        norm_max_ready = sem("norm_max_ready")
        norm_inv_ready = sem("norm_inv_ready")
        q_inv_ready = sem("q_inv_ready")
        qk_unit = sem("qk_unit")
        qk_turned = sem("qk_turned")
        qk_t_ready = sem("qk_t_ready")
        scores_mm = sem("scores_mm")
        max_ready = sem("max_ready")
        neg_ready = sem("neg_ready")
        probs_ready = sem("probs_ready")
        probs_turned = sem("probs_turned")
        probs_t_even = sem("probs_t_even")
        probs_t_odd = sem("probs_t_odd")
        pv_mm = sem("pv_mm")
        sum_inv_ready = sem("sum_inv_ready")
        o_ready = sem("o_ready")
        o_turned = sem("o_turned")
        o_t_ready = sem("o_t_ready")
        fc1_mm = sem("fc1_mm")
        fc1_ready = sem("fc1_ready")

        FIRST = ["cond", "mod_w", "mod_b", "gate_w", "gate_b"]
        SSM = ["in_w1", "xproj_w1", "dt_b", "a_log", "d_skip", "out_w"]
        REST = ["w3", "qkv_w", "row_b", "scale_mul", "proj_w", "fc1_b", "fc2_w"]
        home = dict(cond=cond[:], mod_w=mod_w, mod_b=mod_b[:], gate_w=gate_w, gate_b=gate_b, in_w0=in_w0[:], in_w1=in_w1[:], xproj_w0=xproj_w0[:],
                    xproj_w1=xproj_w1[:],                    dt_b=dt_b[:], a_log=a_log[:], d_skip=d_skip[:], out_w=out_w[:], w12=w12, w3=w3[:], qkv_w=qkv_w[:],
                    row_b=row_b[:], scale_mul=scale_mul[:], proj_w=proj_w[:], fc1_w=fc1_w[:], fc1_b=fc1_b[:], fc2_w=fc2_w[:])
        ROWS = ("gate_b", "row_b", "scale_mul")

        def load(eng, name, signal):
            if name[-1] in "01":
                src = inp[name[:-1]][int(name[-1])]
            else:
                src = inp[name].partition_broadcast(P) if name in ROWS else inp[name]
            if name == "scale_mul":
                src = inp[name][0, :].partition_broadcast(P)
            eng.dma_start(home[name], src).then_inc(signal, 16)

        RES = 4
        x_of = [x_in, x_ssm, x_mlp, x_att, x_out]
        x_rows = inp["x"].rearrange("b (t p) d -> b p t d", p=P)
        out_rows = out.rearrange("b (t p) d -> b p t d", p=P)

        block = ctx.enter_context(nc.Block())

        @block.sync
        def _(sp):
            sp.sem_inc(out_stored, 16)
            for name in FIRST:
                load(sp, name, first_loaded)
            sp.dma_start(x_in[:], x_rows[0]).then_inc(x_loaded, 16)
            load(sp, "in_w0", in0_loaded)
            load(sp, "xproj_w0", xproj0_loaded)
            for name in SSM:
                load(sp, name, ssm_loaded)
            for name in REST:
                load(sp, name, rest_loaded)

            def stack(n):
                sp.wait_ge(bc_ready, (n + 1) * 5)
                for q in range(P // QUAD):
                    for part in range(PARTS):
                        sp.dma_start(bc_stack[part * QUAD:(part + 1) * QUAD, q, :],
                                     bc_parts[q * QUAD:(q + 1) * QUAD, part, :]).then_inc(bc_stacked, 16)

            def turns(b, last):
                stack(b * 2)
                sp.wait_ge(xproj_mm, b * 2 * (KI + 1) + KI + 1)
                load(sp, "w12", w12_loaded)
                sp.dma_start(fc1_w[:], inp["fc1_w"]).then_inc(fc1_loaded, 16)
                stack(b * 2 + 1)
                if not last:
                    sp.wait_ge(res_ready, (b * RES + 1) * 2)
                    sp.dma_start(x_in[:], x_rows[b + 1]).then_inc(x_loaded, 16)
                    sp.wait_ge(mlp_mm, (b + 1) * 2 * KH)
                    load(sp, "xproj_w0", xproj0_loaded)
                    sp.wait_ge(fc1_mm, (b + 1) * KF)
                    load(sp, "in_w0", in0_loaded)
                sp.wait_ge(res_ready, (b * RES + RES) * 2)
                sp.dma_start(out_rows[b], x_out[:]).then_inc(out_stored, 16)

            with sp.Fori(0, B - 1) as b:
                turns(b, False)
            turns(B - 1, True)
            sp.wait_ge(out_stored, 16 * (B + 1))

        @block.gpsimd
        def _(pool):
            pool.memset(ident[:], 0.0).then_inc(ident_zero, 1)
            pool.memset(v_ones[:], 1.0).then_inc(ones_ready, 1)
            pool.wait_ge(ident_zero, 1)
            pool.affine_select(out=ident[:], in_=ident[:], compare_op=ALU.not_equal, fill=1.0, base=0,
                               pattern=[[-1, P]], channel_multiplier=1).then_inc(ident_ready, 1)
            pool.wait_ge(ident_ready, 1)
            for q in range(PARTS):
                rows = slice(q * QUAD, (q + 1) * QUAD)
                pool.tensor_copy(row_pick[rows, :], ident[rows, rows]).then_inc(ident_ready, 1)
                pool.wait_ge(ident_ready, 2 + q)
            pool.wait_ge(ssm_loaded, 16 * len(SSM))
            for d in range(2):
                for k in range(KI):
                    pool.tensor_scalar(d_diag[:, d, k, :], ident[:], d_skip[:, d, k:k + 1], None,
                                       ALU.mult).then_inc(diag_ready, 1)
            pool.sem_inc(read_out, CREDIT)
            with pool.Fori(0, B) as b:
                for d in range(2):
                    n = b * 2 + d
                    for k in range(KI):
                        pool.wait_ge(dt_ready, n * KI + k + 1)
                        pool.tensor_tensor(dtx[:, k, :], dt[:, k, :], xs[:, k, :], ALU.mult).then_inc(dtx_ready, 1)
                    pool.wait_ge(dtx_ready, (n + 1) * KI)
                    pool.sem_inc(wait_over, 1)
                    with pool.Fori(0, NS // 2) as i:
                        for j in range(2):
                            row = n * NS + i * 2 + j
                            pool.wait_ge(c_copied, row + 1 + 2)
                            for k in range(KI):
                                pool.wait_ge(scanned, row * KI + k + 1 + CREDIT)
                                pool.wait_ge(summed, (n + row) * KI + k + 1)
                                pool.tensor_tensor(readout[:, k, :], state[:, k, :], c_rows[:, j, :],
                                                   ALU.mult).then_inc(read_out, 1)
                pool.wait_ge(y_ready, (b + 1) * 2 * KI)
                pool.sem_inc(wait_over, 1)
                pool.memset(qk_pad[:], 0.0).then_inc(pads_ready, 1)
                for t in range(TT):
                    pool.wait_ge(qk_ready, b * TT + t + 1)
                    pool.tensor_tensor(qk_sq[:, t, :], qk[:, t, :], qk[:, t, :], ALU.mult).then_inc(sq_ready, 1)

        @block.scalar
        def _(act):
            act.wait_ge(first_loaded, 16 * len(FIRST))
            act.activation(silu_cond[:], cond[:], ACT.Silu).then_inc(cond_ready, 1)
            act.wait_ge(ssm_loaded, 16 * len(SSM))
            act.activation(a_exp[:], a_log[:], ACT.Exp).then_inc(a_exp_done, 1)
            act.wait_ge(cap_ready, 1)
            act.activation(q_scale[:], scale_cap[:], ACT.Exp).then_inc(q_scale_ready, 1)

            def ln(b, i):
                n = b * 4 + i
                act.wait_ge(ln_var, n + 1)
                act.activation(std[:], var_eps[:], ACT.Sqrt).then_inc(ln_std, 1)
                act.wait_ge(ln_turned, n + 1)
                act.activation(h_t[:, 1, :], banks[1][:], ACT.Identity, bias=mod[:, i, SHIFT, 1, bass.ds(b, 1)],
                               scale=mod[:, i, SCALE, 1, bass.ds(b, 1)]).then_inc(ln_ready, 1)

            act.sem_inc(c_copied, 2)
            act.wait_ge(mod_ready, 2)
            act.wait_ge(gate_ready, 4 * B)
            act.wait_ge(a_ready, 1)
            a_pairs = a_neg[:].rearrange("p d k (j i) -> p d k j i", j=2)
            with act.Fori(0, B) as b:
                ln(b, 0)
                for d in range(2):
                    n = b * 2 + d
                    for m in range(2 * KI):
                        act.wait_ge(in_mm, n * 2 * KI + m + 1)
                        to = xs[:, m, :] if m < KI else silu_z[:, m - KI, :]
                        act.activation(to, banks[m][:], ACT.Silu).then_inc(in_ready, 1)
                    act.preload_act_table_set("natural_log_exp_and_others")
                    for k in range(KI):
                        act.wait_ge(dt_relu, n * KI + k + 1)
                        act.activation(log_part[:, k, :], banks[k][:], ACT.Abs,
                                       bias=dt_b[:, d, k:k + 1]).then_inc(dt_abs, 1)
                    act.wait_ge(dt_abs, (n + 1) * KI)
                    act.activation(log_part[:], log_part[:], ACT.Exp, scale=-1.0).then_inc(dt_exp, 1)
                    act.wait_ge(dt_exp, n + 1)
                    act.activation(log_part[:], log_part[:], ACT.Ln, bias=1.0).then_inc(dt_log, 1)
                    act.wait_ge(dt_ready, (n + 1) * KI)
                    with act.Fori(0, NS // 2) as i:
                        for j in range(2):
                            row = n * NS + i * 2 + j
                            act.wait_ge(bc_spread, row + 1)
                            act.wait_ge(read_out, (row - 1) * KI + CREDIT)
                            act.activation(c_rows[:, j, :], banks[2 + j][:], ACT.Copy).then_inc(c_copied, 1)
                            for k in range(KI):
                                act.wait_ge(scanned, row * KI + k + 1 + CREDIT - RING)
                                act.activation(decay[:, k, :], dt[:, k, :], ACT.Exp,
                                               scale=a_pairs[:, d, k, j, bass.ds(i, 1)]).then_inc(decay_ready, 1)
                ln(b, 1)
                for m in range(KH):
                    act.wait_ge(mlp_mm, (b * KH + m) * 2 + 1)
                    act.activation(silu_a[:, m, :], banks[m][:], ACT.Silu).then_inc(mlp_silu, 1)
                ln(b, 2)
                act.wait_ge(norm_sq_ready, b + 1)
                act.activation(norm[:], norm_sq[:], ACT.Sqrt).then_inc(norm_ready, 1)
                for i in range(0, 2 * NG, 2):
                    act.wait_ge(qk_turned, b * 2 * NG + i + 1)
                    to = q_t[:, i, :] if i < NG else k_t[:, i - NG, :]
                    act.activation(to, banks[i][:], ACT.Copy).then_inc(qk_t_ready, 1)
                for u in range(STEPS):
                    n = b * STEPS + u
                    act.wait_ge(neg_ready, n + 1)
                    for i in range(HG):
                        act.activation(probs[:, i, :], banks[i][:], ACT.Exp,
                                       bias=neg_max[:, u % 2, i:i + 1]).then_inc(probs_ready, 1)
                    for i in range(0, HG, 2):
                        act.wait_ge(probs_turned, n * HG + i + 1)
                        act.activation(probs_t[:, i, :], banks[4 + i % 3][:], ACT.Copy).then_inc(probs_t_even, 1)
                act.wait_ge(o_turned, b + 1)
                act.activation(o_t[:, 1, :], banks[1][:], ACT.Copy).then_inc(o_t_ready, 1)
                ln(b, 3)
                for m in range(KF):
                    act.wait_ge(fc1_mm, b * KF + m + 1)
                    act.activation(gelu_h[:, m, :], banks[m][:], ACT.Gelu, bias=fc1_b[:, m:m + 1]).then_inc(fc1_ready, 1)

        @block.tensor
        def _(pe):
            pe.wait_ge(ident_ready, 1 + PARTS)
            pe.wait_ge(first_loaded, 16 * len(FIRST))
            pe.wait_ge(cond_ready, 1)
            for i in range(4):
                c = cond if i < 2 else silu_cond
                for w in range(2):
                    for f in range(KD):
                        at = ((i * 2 + w) * KD + f) * B
                        for kc in range(KD):
                            last = pe.matmul(banks[0][:, at:at + B], mod_w[:, kc, i, w, f * P:(f + 1) * P], c[:, kc, :],
                                             start=(kc == 0), stop=(kc == KD - 1))
            last.then_inc(mod_mm, 1)
            for b in range(B):
                for g in range(4):
                    c = cond if g < 2 else silu_cond
                    u = b * 4 + g
                    if u >= 4:
                        pe.wait_ge(gate_ready, u - 3)
                    for kc in range(KD):
                        last = pe.matmul(banks[1 + u % 4][:, 0:D], c[:, kc, b:b + 1].to_broadcast([P, P]),
                                         gate_w[:, kc, g, :], start=(kc == 0), stop=(kc == KD - 1))
                    last.then_inc(gate_mm, 1)
            pe.wait_ge(gate_ready, 4 * B)
            pe.wait_ge(mod_ready, 2)
            pe.wait_ge(ssm_loaded, 16 * len(SSM))
            pe.wait_ge(diag_ready, 2 * KI)
            def ln(b, i):
                n = b * 4 + i
                for t in range(TT):
                    pe.wait_ge(ln_norm, n * TT + t + 1)
                    for f in range(KD):
                        last = pe.transpose(banks[f][:, t * P:(t + 1) * P], x_norm[:, t, f * P:(f + 1) * P], ident[:])
                last.then_inc(ln_turned, 1)
                pe.wait_ge(ln_ready, (n + 1) * KD)

            def spread(n, i, j):
                row = n * NS + i * 2 + j
                pe.wait_ge(inflow_ready, (row - 1) * KI + CREDIT)
                pe.wait_ge(c_copied, row + 1)
                pick = row_pick[:, bass.ds(i, 1)].to_broadcast([PARTS * QUAD, P])
                for c in range(2):
                    last = pe.matmul(banks[2 * c + j][:], pick, bc_stack[:, c * NS // QUAD + j, :], start=True, stop=True)
                last.then_inc(bc_spread, 1)

            def sums(n, s, channels):
                row = n * NS + s
                for k in channels:
                    pe.wait_ge(read_out, row * KI + k + 1 + CREDIT)
                    pe.matmul(banks[4 + k][:], ident[:], readout[:, k, :], start=False, stop=True,
                              skip_group_check=True).then_inc(summed, 1)

            def residual_rows(lhs, rhs, steps):
                for t in range(TT):
                    for c in range(steps):
                        last = pe.matmul(banks[t // 2][:, (t % 2) * D:(t % 2 + 1) * D], lhs(c, t), rhs(c),
                                         start=(c == 0), stop=(c == steps - 1))
                    if t % 2:
                        last.then_inc(res_mm, 1)

            with pe.Fori(0, B) as b:
                ln(b, 0)
                for d in range(2):
                    n = b * 2 + d
                    if d == 1:
                        pe.wait_ge(y_ready, n * KI)
                    else:
                        pe.wait_ge(in0_loaded, 16 * (b + 1))
                        pe.wait_ge(xproj0_loaded, 16 * (b + 1))
                    for m in range(2 * KI):
                        for kc in range(KD):
                            last = pe.matmul(banks[m][:], in_w[d][:, kc, m * P:(m + 1) * P], h_t[:, kc, :],
                                             start=(kc == 0), stop=(kc == KD - 1))
                        last.then_inc(in_mm, 1)
                    pe.wait_ge(in_ready, (n + 1) * 2 * KI)
                    for m in range(KI + 1):
                        for kc in range(KI):
                            last = pe.matmul(banks[m][:], xproj_w[d][:, kc, m * P:(m + 1) * P], xs[:, kc, :],
                                             start=(kc == 0), stop=(kc == KI - 1))
                        last.then_inc(xproj_mm, 1)
                    pe.wait_ge(bc_stacked, (n + 1) * 16 * PARTS * P // QUAD)
                    pe.wait_ge(dt_abs, (n + 1) * KI)
                    pe.wait_ge(dt_relu, (n + 1) * KI)
                    for k in range(KI):
                        pe.matmul(banks[4 + k][:], d_diag[:, d, k, :], xs[:, k, :], start=True,
                                  stop=True).then_inc(summed, 1)
                    spread(n, 0, 0)
                    spread(n, 0, 1)
                    with pe.Fori(0, NS // 2 - 1) as i:
                        for j in range(2):
                            sums(n, i * 2 + j, range(KI - 1))
                            spread(n, i + 1, j)
                            sums(n, i * 2 + j, range(KI - 1, KI))
                    for j in range(2):
                        sums(n, NS - 2 + j, range(KI))
                pe.wait_ge(y_ready, (b + 1) * 2 * KI)
                residual_rows(lambda c, t: y_gated[:, c // KI, c % KI, t * P:(t + 1) * P],
                              lambda c: out_w[:, c // KI, c % KI, :], 2 * KI)
                ln(b, 1)
                pe.wait_ge(rest_loaded, 16 * len(REST))
                pe.wait_ge(w12_loaded, 16 * (b + 1))
                for m in range(KH):
                    for w in range(2):
                        for kc in range(KD):
                            last = pe.matmul(banks[m + w * KH][:], w12[:, w, kc, m * P:(m + 1) * P], h_t[:, kc, :],
                                             start=(kc == 0), stop=(kc == KD - 1))
                        last.then_inc(mlp_mm, 1)
                pe.wait_ge(mlp_ready, (b + 1) * KH)
                residual_rows(lambda c, t: ab[:, c, t * P:(t + 1) * P], lambda c: w3[:, c, :], KH)
                ln(b, 2)
                for t in range(TT):
                    for kc in range(KD):
                        pe.matmul(banks[t][:], h_t[:, kc, t * P:(t + 1) * P], qkv_w[:, kc, 0:2 * D],
                                  start=(kc == 0), stop=(kc == KD - 1))
                    for kc in range(KD):
                        last = pe.matmul(banks[4 + t][:, 0:D], h_t[:, kc, t * P:(t + 1) * P], qkv_w[:, kc, 2 * D:3 * D],
                                         start=(kc == 0), stop=(kc == KD - 1))
                    last.then_inc(qkv_mm, 1)
                pe.wait_ge(v_ready, (b + 1) * TT)
                for i in range(2 * NG):
                    for t in range(TT):
                        pe.wait_ge(qk_unit, b * TT + t + 1)
                        last = pe.transpose(banks[i][:, t * P:(t + 1) * P], qk_pad[:, t, i, :], ident[:])
                    last.then_inc(qk_turned, 1)
                pe.wait_ge(qk_t_ready, (b + 1) * 2 * NG)

                def scores(t, g):
                    n = b * STEPS + t * NG + g
                    if t or g:
                        pe.wait_ge(probs_ready, n * HG)
                    for i in range(HG):
                        a = slice(i * LANE, i * LANE + HD)
                        last = pe.matmul(banks[i][:], q_t[a, g, t * P:(t + 1) * P], k_t[a, g, :], start=True, stop=True)
                    last.then_inc(scores_mm, 1)

                def turn(t, g):
                    n = b * STEPS + t * NG + g
                    for i in range(HG):
                        pe.wait_ge(probs_ready, n * HG + i + 1)
                        if i == 3:
                            pe.wait_ge(probs_t_even, n * 2 + 1)
                        for kt in range(TT):
                            last = pe.transpose(banks[4 + i % 3][:, kt * P:(kt + 1) * P],
                                                probs[:, i, kt * P:(kt + 1) * P], ident[:])
                        last.then_inc(probs_turned, 1)

                def weigh(t, g):
                    n = b * STEPS + t * NG + g
                    pe.wait_ge(probs_t_even, (n + 1) * 2)
                    pe.wait_ge(probs_t_odd, (n + 1) * 2)
                    if t or g:
                        pe.wait_ge(o_ready, n)
                    for i in range(HG):
                        for kt in range(TT):
                            last = pe.matmul(banks[7][:, i * VW:(i + 1) * VW], probs_t[:, i, kt * P:(kt + 1) * P],
                                             v_ones[:, kt, g * HG + i, :], start=(kt == 0), stop=(kt == TT - 1))
                    last.then_inc(pv_mm, 1)

                steps = [(t, g) for t in range(TT) for g in range(NG)]
                scores(*steps[0])
                for u, step in enumerate(steps):
                    turn(*step)
                    if step != steps[-1]:
                        scores(*steps[u + 1])
                    weigh(*step)
                pe.wait_ge(o_ready, (b + 1) * STEPS)
                for t in range(TT):
                    for f in range(KD):
                        last = pe.transpose(banks[f][:, t * P:(t + 1) * P], o_rows[:, t, f * P:(f + 1) * P], ident[:])
                last.then_inc(o_turned, 1)
                pe.wait_ge(o_t_ready, (b + 1) * KD)
                residual_rows(lambda c, t: o_t[:, c, t * P:(t + 1) * P], lambda c: proj_w[:, c, :], KD)
                ln(b, 3)
                pe.wait_ge(fc1_loaded, 16 * (b + 1))
                for m in range(KF):
                    for kc in range(KD):
                        last = pe.matmul(banks[m][:], fc1_w[:, kc, m * P:(m + 1) * P], h_t[:, kc, :],
                                         start=(kc == 0), stop=(kc == KD - 1))
                    last.then_inc(fc1_mm, 1)
                pe.wait_ge(fc1_ready, (b + 1) * KF)
                residual_rows(lambda c, t: gelu_h[:, c, t * P:(t + 1) * P], lambda c: fc2_w[:, c, :], KF)

        @block.vector
        def _(dve):
            dve.wait_ge(first_loaded, 16 * len(FIRST))
            dve.wait_ge(mod_mm, 1)
            dve.tensor_tensor(mod[:].rearrange("p i w f b -> p (i w f) b"),
                              banks[0][:, 0:16 * B].rearrange("p (g b) -> p g b", b=B),
                              mod_b[:].rearrange("p i w f -> p (i w f)").unsqueeze(2).to_broadcast([P, 16, B]),
                              ALU.add).then_inc(mod_sum, 1)
            dve.wait_ge(mod_sum, 1)
            one_plus = mod[:, :, SCALE, :, :].rearrange("p i f b -> p i (f b)")
            dve.tensor_scalar(one_plus, one_plus, 1.0, None, ALU.add).then_inc(mod_ready, 2)
            for b in range(B):
                for g in range(4):
                    u = b * 4 + g
                    dve.wait_ge(gate_mm, u + 1)
                    dve.tensor_tensor(gate[:, b, g, :], banks[1 + u % 4][:, 0:D], gate_b[:, g, :],
                                      ALU.add).then_inc(gate_ready, 1)
            dve.wait_ge(a_exp_done, 1)
            dve.tensor_scalar(a_neg[:], a_exp[:], -1.0, None, ALU.mult).then_inc(a_ready, 1)
            dve.wait_ge(rest_loaded, 16 * len(REST))
            dve.tensor_scalar(scale_cap[:], scale_mul[:], MAX_SCALE_MUL, None, ALU.min).then_inc(cap_ready, 1)
            dve.wait_ge(gate_ready, 4 * B)
            dve.wait_ge(mod_ready, 2)
            dve.wait_ge(ones_ready, 1)
            dve.wait_ge(q_scale_ready, 1)
            dve.sem_inc(inflow_ready, CREDIT)
            dve.sem_inc(scanned, CREDIT)

            def ln(b, i, x, eps):
                n = b * 4 + i
                if i:
                    dve.wait_ge(res_ready, (b * RES + i) * 2)
                for t in range(TT):
                    dve.bn_stats(stats[:, t, :], x[:, t, :]).then_inc(ln_stat, 1)
                dve.wait_ge(ln_stat, (n + 1) * TT)
                dve.sem_inc(wait_over, 1)
                for t in range(TT):
                    dve.bn_aggr(mean_var[:, t, :], stats[:, t, :]).then_inc(ln_aggr, 1)
                dve.wait_ge(ln_aggr, (n + 1) * TT)
                dve.tensor_scalar(var_eps[:], mean_var[:, :, 1], eps, None, ALU.add).then_inc(ln_var, 1)
                dve.wait_ge(ln_std, n + 1)
                dve.reciprocal(rstd[:], std[:]).then_inc(ln_rstd, 1)
                dve.wait_ge(ln_rstd, n + 1)
                for t in range(TT):
                    dve.tensor_scalar(x_norm[:, t, :], x[:, t, :], mean_var[:, t, 0:1], rstd[:, t:t + 1],
                                      ALU.subtract, ALU.mult).then_inc(ln_norm, 1)
                dve.wait_ge(ln_turned, n + 1)
                dve.tensor_scalar(h_t[:, 0, :], banks[0][:], mod[:, i, SCALE, 0, bass.ds(b, 1)], mod[:, i, SHIFT, 0, bass.ds(b, 1)],
                                  ALU.mult, ALU.add).then_inc(ln_ready, 1)

            def residual(b, i, g, bias=None):
                for p in range(2):
                    n = (b * RES + i) * 2 + p
                    tiles = slice(2 * p, 2 * p + 2)
                    dve.wait_ge(res_mm, n + 1)
                    src = banks[p][:].rearrange("p (t d) -> p t d", d=D)
                    if bias is not None:
                        dve.tensor_tensor(biased[:, tiles, :], src, row_b[:, bias:bias + 1, :].to_broadcast([P, 2, D]),
                                          ALU.add).then_inc(res_biased, 1)
                        dve.wait_ge(res_biased, b * 4 + (2 if i == 3 else 0) + p + 1)
                        src = biased[:, tiles, :]
                    dve.tensor_tensor(gated[:, tiles, :], src, gate[:, b, g, :].unsqueeze(1).to_broadcast([P, 2, D]),
                                      ALU.mult).then_inc(res_gated, 1)
                    dve.wait_ge(res_gated, n + 1)
                    dve.tensor_tensor(x_of[i + 1][:, tiles, :], x_of[i][:, tiles, :], gated[:, tiles, :],
                                      ALU.add).then_inc(res_ready, 1)

            with dve.Fori(0, B) as b:
                dve.wait_ge(x_loaded, (b + 1) * 16)
                ln(b, 0, x_in, EPS_MAMBA)
                for d in range(2):
                    n = b * 2 + d
                    for k in range(KI):
                        dve.wait_ge(xproj_mm, n * (KI + 1) + k + 1)
                        dve.tensor_scalar(dt[:, k, :], banks[k][:], dt_b[:, d, k:k + 1], 0.0,
                                          ALU.add, ALU.max).then_inc(dt_relu, 1)
                    dve.wait_ge(xproj_mm, (n + 1) * (KI + 1))
                    dve.tensor_copy(bc_parts[:, 0, :], banks[KI][:]).then_inc(bc_ready, 1)
                    dve.wait_ge(bc_ready, n * 5 + 1)
                    dve.tensor_tensor(bc_rest[:], banks[KI][:], bc_parts[:, 0, :], ALU.subtract).then_inc(bc_ready, 1)
                    dve.wait_ge(bc_ready, n * 5 + 2)
                    dve.tensor_copy(bc_parts[:, 1, :], bc_rest[:]).then_inc(bc_ready, 1)
                    dve.wait_ge(bc_ready, n * 5 + 3)
                    dve.tensor_tensor(bc_rest[:], bc_rest[:], bc_parts[:, 1, :], ALU.subtract).then_inc(bc_ready, 1)
                    dve.wait_ge(bc_ready, n * 5 + 4)
                    dve.tensor_copy(bc_parts[:, 2, :], bc_rest[:]).then_inc(bc_ready, 1)
                    dve.wait_ge(dt_log, n + 1)
                    dve.wait_ge(dt_relu, (n + 1) * KI)
                    for k in range(KI):
                        dve.tensor_tensor(dt[:, k, :], dt[:, k, :], log_part[:, k, :], ALU.add).then_inc(dt_ready, 1)
                    dve.wait_ge(dtx_ready, (n + 1) * KI)
                    dve.sem_inc(wait_over, 1)
                    time = slice(None, None, -1) if d else slice(None)

                    def inflow_of(row, j, k):
                        dve.tensor_tensor(inflow[:, k, :], dtx[:, k, :], banks[j][:], ALU.mult).then_inc(inflow_ready, 1)

                    def scan(row, k):
                        unit = row * KI + k
                        dve.wait_ge(decay_ready, unit + 1)
                        dve.wait_ge(inflow_ready, unit + 1 + CREDIT)
                        dve.wait_ge(read_out, unit + 1 + CREDIT - RING)
                        dve.tensor_tensor_scan(state[:, k, time], decay[:, k, time], inflow[:, k, time], 0.0,
                                               ALU.mult, ALU.add).then_inc(scanned, 1)

                    with dve.Fori(0, NS // 2) as i:
                        for j in range(2):
                            row = n * NS + i * 2 + j
                            dve.wait_ge(bc_spread, row + 1)
                            for k in range(KI):
                                dve.wait_ge(scanned, row * KI + k + 1 + CREDIT - RING)
                                inflow_of(row, j, k)
                                if k:
                                    scan(row, k - 1)
                            scan(row, KI - 1)
                    for k in range(KI):
                        dve.wait_ge(summed, ((n + 1) * (NS + 1) - 1) * KI + k + 1)
                        dve.tensor_tensor(y_gated[:, d, k, :], banks[4 + k][:], silu_z[:, k, :],
                                          ALU.mult).then_inc(y_ready, 1)
                residual(b, 0, GATE_MAMBA)
                ln(b, 1, x_ssm, EPS_MAMBA)
                dve.wait_ge(out_stored, 16 * (b + 1))
                for m in range(KH):
                    dve.wait_ge(mlp_silu, b * KH + m + 1)
                    dve.wait_ge(mlp_mm, (b * KH + m + 1) * 2)
                    dve.tensor_tensor(ab[:, m, :], banks[4 + m][:], silu_a[:, m, :], ALU.mult).then_inc(mlp_ready, 1)
                residual(b, 1, GATE_MLP)
                ln(b, 2, x_mlp, EPS_LN)
                for t in range(TT):
                    dve.wait_ge(qkv_mm, b * TT + t + 1)
                    dve.tensor_tensor(qk[:, t, 0:D], banks[t][:, 0:D], row_b[:, Q_BIAS, :], ALU.add)
                    dve.tensor_copy(qk[:, t, D:2 * D], banks[t][:, D:2 * D]).then_inc(qk_ready, 1)
                    dve.tensor_tensor(v_ones[:, t, :, 0:HD], banks[4 + t][:, 0:D].rearrange("p (h e) -> p h e", e=HD),
                                      row_b[:, V_BIAS, :].rearrange("p (h e) -> p h e", e=HD),
                                      ALU.add).then_inc(v_ready, 1)
                dve.wait_ge(sq_ready, (b + 1) * TT)
                dve.tensor_reduce(norm_sq[:], qk_sq.rearrange("p t (h e) -> p t h e", e=HD), AX.X,
                                  ALU.add).then_inc(norm_sq_ready, 1)
                dve.wait_ge(norm_ready, b + 1)
                dve.tensor_scalar(norm_max[:], norm[:], EPS_NORM, None, ALU.max).then_inc(norm_max_ready, 1)
                dve.wait_ge(norm_max_ready, b + 1)
                dve.reciprocal(norm_inv[:], norm_max[:]).then_inc(norm_inv_ready, 1)
                dve.wait_ge(norm_inv_ready, b + 1)
                dve.tensor_tensor(norm_inv[:, :, 0:H], norm_inv[:, :, 0:H],
                                  q_scale[:].unsqueeze(1).to_broadcast([P, TT, H]), ALU.mult).then_inc(q_inv_ready, 1)
                dve.wait_ge(q_inv_ready, b + 1)
                dve.wait_ge(pads_ready, b + 1)
                for t in range(TT):
                    pad = qk_pad[:, t, :, :].rearrange("p g (h e) -> p (g h) e", e=LANE)
                    dve.tensor_tensor(pad[:, :, 0:HD], qk[:, t, :].rearrange("p (h e) -> p h e", e=HD),
                                      norm_inv[:, t, :].unsqueeze(2).to_broadcast([P, 2 * H, HD]),
                                      ALU.mult).then_inc(qk_unit, 1)
                for i in range(1, 2 * NG, 2):
                    dve.wait_ge(qk_turned, b * 2 * NG + i + 1)
                    to = q_t[:, i, :] if i < NG else k_t[:, i - NG, :]
                    dve.tensor_copy(to, banks[i][:]).then_inc(qk_t_ready, 1)

                def maxima(u):
                    n = b * STEPS + u
                    dve.wait_ge(scores_mm, n + 1)
                    for i in range(HG):
                        last = dve.tensor_reduce(row_max[:, u % 2, i:i + 1], banks[i][:], AX.X, ALU.max)
                    last.then_inc(max_ready, 1)
                    dve.wait_ge(max_ready, n + 1)
                    dve.tensor_scalar(neg_max[:, u % 2, :], row_max[:, u % 2, :], -1.0, None, ALU.mult).then_inc(neg_ready, 1)

                def divide(u):
                    n = b * STEPS + u
                    t, g = u // NG, u % NG
                    o = banks[7][:, 0:HG * VW].rearrange("p (i e) -> p i e", e=VW)
                    dve.wait_ge(pv_mm, n + 1)
                    dve.reciprocal(sum_inv[:, u % 2, :], o[:, :, HD]).then_inc(sum_inv_ready, 1)
                    dve.wait_ge(sum_inv_ready, n + 1)
                    dve.tensor_tensor(o_rows[:, t, g * HG * HD:(g + 1) * HG * HD].rearrange("p (i e) -> p i e", e=HD),
                                      o[:, :, 0:HD], sum_inv[:, u % 2, :].unsqueeze(2).to_broadcast([P, HG, HD]),
                                      ALU.mult).then_inc(o_ready, 1)

                maxima(0)
                for u in range(STEPS):
                    for i in range(1, HG, 2):
                        dve.wait_ge(probs_turned, (b * STEPS + u) * HG + i + 1)
                        dve.tensor_copy(probs_t[:, i, :], banks[4 + i % 3][:]).then_inc(probs_t_odd, 1)
                    if u + 1 < STEPS:
                        maxima(u + 1)
                    divide(u)
                dve.wait_ge(o_turned, b + 1)
                dve.tensor_copy(o_t[:, 0, :], banks[0][:]).then_inc(o_t_ready, 1)
                residual(b, 2, GAMMA1, PROJ_B)
                ln(b, 3, x_att, EPS_LN)
                residual(b, 3, GAMMA2, FC2_B)


def kernel(**inputs):
    import numpy as np
    import concourse.bacc as bacc
    from concourse.bass_utils import run_bass_kernel_spmd

    a = {k: np.asarray(v) for k, v in inputs.items()}

    def cut(w):
        return w.reshape(-1, P, *w.shape[1:]).swapaxes(0, 1)

    mamba_w, mlp_w, ada_w = a["L0_cond_adaln_mamba_w"], a["L0_cond_adaln_mlp_w"], a["L1_cond_ada_w"].T
    mamba_b, mlp_b, ada_b = a["L0_cond_adaln_mamba_b"], a["L0_cond_adaln_mlp_b"], a["L1_cond_ada_b"]

    def col(w, i):
        return w[..., i * D:(i + 1) * D]

    pairs_w = [(col(mamba_w, 0), col(mamba_w, 1)), (col(mlp_w, 0), col(mlp_w, 1)),
               (col(ada_w, 4), col(ada_w, 2)), (col(ada_w, 5), col(ada_w, 3))]
    pairs_b = [(col(mamba_b, 0), col(mamba_b, 1)), (col(mlp_b, 0), col(mlp_b, 1)),
               (col(ada_b, 4), col(ada_b, 2)), (col(ada_b, 5), col(ada_b, 3))]
    gates_w = [col(mamba_w, 2), col(mlp_w, 2), col(ada_w, 0), col(ada_w, 1)]
    gates_b = [col(mamba_b, 2), col(mlp_b, 2), col(ada_b, 0), col(ada_b, 1)]

    def both(name):
        return np.stack([cut(a[f"L0_cond_{d}_{name}"]) for d in ("fwd", "bwd")], 1)

    laid = {
        "x": a["x"],
        "cond": cut(a["cond_1024"].T),
        "mod_w": cut(np.stack([np.stack(p, 1) for p in pairs_w], 1)),
        "mod_b": np.stack([np.stack([v.reshape(KD, P).T for v in p], 1) for p in pairs_b], 1),
        "gate_w": cut(np.stack(gates_w, 1)),
        "gate_b": np.stack(gates_b, 0),
        "in_w": both("in_w").swapaxes(0, 1),
        "xproj_w": both("xproj_w").swapaxes(0, 1),
        "dt_b": both("dt_bias"),
        "a_log": both("A_log"),
        "d_skip": both("D"),
        "out_w": both("out_w"),
        "w12": np.stack([cut(a["L0_cond_mlp_w1"]), cut(a["L0_cond_mlp_w2"])], 1),
        "w3": cut(a["L0_cond_mlp_w3"]),
        "qkv_w": cut(a["L1_cond_mat_qkv_w"].T),
        "row_b": np.stack([a[f"L1_cond_{v}"] for v in ("q_bias", "v_bias", "proj_b", "fc2_b")], 0),
        "scale_mul": a["L1_cond_scale_mul"].reshape(1, H),
        "proj_w": cut(a["L1_cond_proj_w"].T),
        "fc1_w": cut(a["L1_cond_fc1_w"].T),
        "fc1_b": cut(a["L1_cond_fc1_b"]),
        "fc2_w": cut(a["L1_cond_fc2_w"].T),
    }
    nc = bacc.Bacc("TRN2", target_bir_lowering=False, num_devices=1)
    arrays, aps = {}, {}
    for name, shape in INPUTS.items():
        arrays[f"in_{name}"] = np.ascontiguousarray(laid[name]).reshape(shape)
        aps[name] = nc.dram_tensor(f"in_{name}", shape, F32, kind="ExternalInput").ap()
    out = nc.dram_tensor("out", [B, L, D], F32, kind="ExternalOutput").ap()
    build(nc, aps, out)
    r = run_bass_kernel_spmd(nc, [arrays], core_ids=[0])
    return r.results[0]["out"]
```

```python
from contextlib import ExitStack

import concourse.bass as bass
from concourse import mybir

F32 = mybir.dt.float32
BF16 = mybir.dt.bfloat16
ALU = mybir.AluOpType
ACT = mybir.ActivationFunctionType
AX = mybir.AxisListType

P = 128
B = 4
L = 512
D = 256
DI = 512
NS = 64
HID = 512
FF = 1024
H = 16
HD = D // H
TT = L // P
KD = D // P
KI = DI // P
KH = HID // P
KF = FF // P
LANE = 32
HG = P // LANE
NG = H // HG
STEPS = TT * NG
PARTS = 3
QUAD = 32
RING = 4
CREDIT = RING + 1
POOL_PAIR = 2 * KI - 1
KV = 3
KA = KI - KV
ORDER = list(range(KV, KI)) + list(range(KV))
WA = KA * P
TURN_CREDIT = 2 * KA + 1
FLOW_CREDIT = KV + 1
EPS_MAMBA = 1e-5
EPS_LN = 1e-6
EPS_NORM = 1e-12
MAX_SCALE_MUL = 4.605170185988092
SHIFT, SCALE = 0, 1
GATE_MAMBA, GATE_MLP, GAMMA1, GAMMA2 = range(4)
Q_BIAS, V_BIAS, PROJ_B, FC2_B = range(4)

INPUTS = {
    "x": [B, L, D],
    "cond": [P, KD, B],
    "mod_w": [P, KD, 4, 2, D],
    "mod_b": [P, 4, 2, KD],
    "gate_w": [P, KD, 4, D],
    "gate_b": [4, D],
    "in_w": [2, P, KD, 2 * DI],
    "xproj_w": [2, P, KI, DI + 2 * NS],
    "dt_b": [P, 2, KI],
    "a_log": [P, 2, KI, NS],
    "d_skip": [P, 2, KI],
    "out_w": [P, 2, KI, D],
    "w12": [P, 2, KD, HID],
    "w3": [P, KH, D],
    "qkv_w": [P, KD, 3 * D],
    "row_b": [4, D],
    "scale_mul": [1, H],
    "proj_w": [P, KD, D],
    "fc1_w": [P, KD, FF],
    "fc1_b": [P, KF],
    "fc2_w": [P, KF, D],
}


def build(nc, inp, out):
    ctx = ExitStack()
    with ctx:
        def sb(name, shape, dtype=F32):
            return ctx.enter_context(nc.sbuf_tensor(name, shape, dtype))

        def sem(name):
            return ctx.enter_context(nc.semaphore(name))

        ident = sb("ident", [P, P])
        row_pick = sb("row_pick", [PARTS * QUAD, QUAD], BF16)
        cond = sb("cond", [P, KD, B])
        silu_cond = sb("silu_cond", [P, KD, B])
        mod_b = sb("mod_b", [P, 4, 2, KD])
        mod = sb("mod", [P, 4, 2, KD, B])
        gate = sb("gate", [P, B, 4, D])
        in_w0 = sb("in_w0", [P, KD, 2 * DI])
        in_w1 = sb("in_w1", [P, KD, 2 * DI])
        in_w = [in_w0, in_w1]
        fc1_w = in_w0
        xproj_w0 = sb("xproj_w0", [P, KI, DI + 2 * NS])
        xproj_w1 = sb("xproj_w1", [P, KI, DI + 2 * NS])
        xproj_w = [xproj_w0, xproj_w1]
        w12 = xproj_w0[:].rearrange("p k n -> p (k n)")[:, 0:2 * KD * HID].rearrange("p (w k n) -> p w k n", w=2, k=KD)
        dt_b = sb("dt_b", [P, 2, KI])
        a_log = sb("a_log", [P, 2, KI, NS])
        a_exp = sb("a_exp", [P, 2, KI, NS])
        a_neg = sb("a_neg", [P, 2, KI, NS])
        d_skip = sb("d_skip", [P, 2, KI])
        d_diag = sb("d_diag", [P, 2, KI, P])
        out_w = sb("out_w", [P, 2, KI, D])
        w3 = sb("w3", [P, KH, D])
        qkv_w = sb("qkv_w", [P, KD, 3 * D])
        row_b = sb("row_b", [P, 4, D])
        scale_mul = sb("scale_mul", [P, H])
        scale_cap = sb("scale_cap", [P, H])
        q_scale = sb("q_scale", [P, H])
        proj_w = sb("proj_w", [P, KD, D])
        fc1_b = sb("fc1_b", [P, KF])
        fc2_w = sb("fc2_w", [P, KF, D])

        x_in = sb("x_in", [P, TT, D])
        x_ssm = sb("x_ssm", [P, TT, D])
        x_mlp = sb("x_mlp", [P, TT, D])
        x_att = x_ssm
        x_out = x_mlp
        stats = sb("stats", [P, TT, 6])
        mean_var = sb("mean_var", [P, TT, 2])
        var_eps = sb("var_eps", [P, TT])
        std = sb("std", [P, TT])
        rstd = sb("rstd", [P, TT])
        x_norm = sb("x_norm", [P, TT, D])
        h_t = sb("h_t", [P, KD, L])
        xs = sb("xs", [P, KI, L])
        silu_z = sb("silu_z", [P, KI, L])
        dt = sb("dt", [P, KI, L])
        dtx = sb("dtx", [P, KI, L])
        bc_rest = sb("bc_rest", [P, L])
        bc_parts = sb("bc_parts", [P, PARTS, L], BF16)
        bc_stack = sb("bc_stack", [PARTS * QUAD, P // QUAD, L], BF16)
        y_gated = sb("y_gated", [P, 2, KI, L])
        scan_in = sb("scan_in", [P, 2 * RING, L])
        decay = scan_in[:, 0:RING, :]
        inflow = scan_in[:, RING:RING + KV, :]
        state = sb("state", [P, RING, L])
        c_rows = sb("c_rows", [P, 2, L])
        log_part = state
        readout = xs

        mod_w = y_gated[:, :, :, :].rearrange("p a k l -> p (a k l)").rearrange("p (k i w d) -> p k i w d", k=KD, i=4, w=2)
        gate_w = log_part[:, :, :].rearrange("p k l -> p (k l)").rearrange("p (k g d) -> p k g d", k=KD, g=4)
        gate_b = c_rows[:, :, :].rearrange("p a (g d) -> p (a g) d", d=D)

        b_tok = sb("b_tok", [P, TT, NS])
        dtx_tok = x_norm[:].rearrange("p t d -> p (t d)")[:, 0:TT * WA].rearrange("p (t c) -> p t c", c=WA)
        inflow_tok = [x[:].rearrange("p t d -> p (t d)")[:, 0:TT * WA].rearrange("p (t c) -> p t c", c=WA)
                      for x in (x_ssm, x_mlp)]

        gated = x_norm
        o_lanes = bc_rest[:].rearrange("p (u q) -> p u q", q=P)[:, 0:2, :]
        qk = xs[:, :, :]
        qk_sq = state[:, :, :]
        v_ones = silu_z[:].rearrange("p k (h e) -> p k h e", e=LANE)
        qk_pad = scan_in[:, :, :].rearrange("p r l -> p (r l)").rearrange("p (t g c) -> p t g c", t=TT, g=2 * NG)
        norm_sq = sb("norm_sq", [P, TT, 2 * H])
        norm = sb("norm", [P, TT, 2 * H])
        norm_max = sb("norm_max", [P, TT, 2 * H])
        norm_inv = sb("norm_inv", [P, TT, 2 * H])
        q_t = dt[:, :, :]
        k_t = dtx[:, :, :]
        neg_max = sb("neg_max", [P, 2, HG])
        probs = y_gated[:, 0, :, :]
        probs_t = [[y_gated[:, 1, i, :] for i in range(HG)],
                   [h_t[:, 0, :], h_t[:, 1, :]] +
                   [x_norm[:].rearrange("p t d -> p (t d)")[:, i * L:(i + 1) * L] for i in range(2)]]
        sum_inv = sb("sum_inv", [P, 2, HG])
        o_rows = state[:, 0:2, :].rearrange("p r l -> p (r l)").rearrange("p (t d) -> p t d", d=D)
        o_t = state[:, 2:2 + KD, :]
        biased = dt[:, 0:2, :].rearrange("p r l -> p (r l)").rearrange("p (t d) -> p t d", d=D)
        silu_a = log_part[:, :, :]
        ab = xs[:, :, :]
        gelu_h = y_gated[:, :, :, :].rearrange("p a k l -> p (a k) l")

        banks = [ctx.enter_context(nc.psum_tensor(f"bank{i}", [P, 512], F32)) for i in range(8)]

        first_loaded = sem("first_loaded")
        ssm_loaded = sem("ssm_loaded")
        rest_loaded = sem("rest_loaded")
        x_loaded = sem("x_loaded")
        w12_loaded = sem("w12_loaded")
        fc1_loaded = sem("fc1_loaded")
        xproj0_loaded = sem("xproj0_loaded")
        in0_loaded = sem("in0_loaded")
        out_stored = sem("out_stored")
        wait_over = sem("wait_over")
        ident_zero = sem("ident_zero")
        ident_ready = sem("ident_ready")
        ones_ready = sem("ones_ready")
        pads_ready = sem("pads_ready")
        diag_ready = sem("diag_ready")
        cond_ready = sem("cond_ready")
        a_exp_done = sem("a_exp_done")
        a_ready = sem("a_ready")
        cap_ready = sem("cap_ready")
        q_scale_ready = sem("q_scale_ready")
        mod_mm = sem("mod_mm")
        mod_sum = sem("mod_sum")
        mod_ready = sem("mod_ready")
        gate_mm = sem("gate_mm")
        gate_ready = sem("gate_ready")
        ln_stat = sem("ln_stat")
        ln_aggr = sem("ln_aggr")
        ln_var = sem("ln_var")
        ln_std = sem("ln_std")
        ln_rstd = sem("ln_rstd")
        ln_norm = sem("ln_norm")
        ln_turned = sem("ln_turned")
        ln_ready = sem("ln_ready")
        in_mm = sem("in_mm")
        in_ready = sem("in_ready")
        xproj_mm = sem("xproj_mm")
        dt_relu = sem("dt_relu")
        dt_abs = sem("dt_abs")
        dt_exp = sem("dt_exp")
        dt_log = sem("dt_log")
        dt_ready = sem("dt_ready")
        dtx_ready = sem("dtx_ready")
        bc_ready = sem("bc_ready")
        b_tok_mm = sem("b_tok_mm")
        b_tok_ready = sem("b_tok_ready")
        dtx_turned = sem("dtx_turned")
        dtx_tok_ready = sem("dtx_tok_ready")
        inflow_tok_ready = sem("inflow_tok_ready")
        inflow_turned = sem("inflow_turned")
        bc_stacked = sem("bc_stacked")
        bc_spread = sem("bc_spread")
        c_copied = sem("c_copied")
        decay_ready = sem("decay_ready")
        inflow_ready = sem("inflow_ready")
        scanned = sem("scanned")
        read_out = sem("read_out")
        read_out_dve = sem("read_out_dve")
        summed = sem("summed")
        y_ready = sem("y_ready")
        res_mm = sem("res_mm")
        res_biased = sem("res_biased")
        res_gated = sem("res_gated")
        res_ready = sem("res_ready")
        mlp_mm = sem("mlp_mm")
        mlp_silu = sem("mlp_silu")
        mlp_ready = sem("mlp_ready")
        qkv_mm = sem("qkv_mm")
        qk_ready = sem("qk_ready")
        v_ready = sem("v_ready")
        sq_ready = sem("sq_ready")
        norm_sq_ready = sem("norm_sq_ready")
        norm_ready = sem("norm_ready")
        norm_max_ready = sem("norm_max_ready")
        norm_inv_ready = sem("norm_inv_ready")
        q_inv_ready = sem("q_inv_ready")
        qk_unit = sem("qk_unit")
        qk_turned = sem("qk_turned")
        qk_t_ready = sem("qk_t_ready")
        scores_mm = sem("scores_mm")
        neg_ready = sem("neg_ready")
        probs_ready = sem("probs_ready")
        probs_turned = sem("probs_turned")
        probs_t_even = sem("probs_t_even")
        probs_t_odd = sem("probs_t_odd")
        pv_mm = sem("pv_mm")
        sum_inv_ready = sem("sum_inv_ready")
        lanes_ready = sem("lanes_ready")
        lanes_turned = sem("lanes_turned")
        o_ready = sem("o_ready")
        o_turned = sem("o_turned")
        o_t_ready = sem("o_t_ready")
        fc1_mm = sem("fc1_mm")
        fc1_ready = sem("fc1_ready")

        FIRST = ["cond", "mod_w", "mod_b", "gate_w", "gate_b"]
        SSM = ["in_w1", "xproj_w1", "dt_b", "a_log", "d_skip", "out_w"]
        REST = ["w3", "qkv_w", "row_b", "scale_mul", "proj_w", "fc1_b", "fc2_w"]
        home = dict(cond=cond[:], mod_w=mod_w, mod_b=mod_b[:], gate_w=gate_w, gate_b=gate_b, in_w0=in_w0[:], in_w1=in_w1[:], xproj_w0=xproj_w0[:],
                    xproj_w1=xproj_w1[:], dt_b=dt_b[:], a_log=a_log[:], d_skip=d_skip[:], out_w=out_w[:],
                    w12=w12, w3=w3[:], qkv_w=qkv_w[:],
                    row_b=row_b[:], scale_mul=scale_mul[:], proj_w=proj_w[:], fc1_w=fc1_w[:], fc1_b=fc1_b[:], fc2_w=fc2_w[:])
        ROWS = ("gate_b", "row_b", "scale_mul")

        def wait_readout(eng, n, i, j, k):
            pair = n * (NS // 2) + i
            if j and k == 0:
                eng.wait_ge(read_out_dve, pair + 1 + 2)
            else:
                eng.wait_ge(read_out, pair * POOL_PAIR + j * (KI - 1) + k + 1 + 2 * KI)

        def wait_readouts_before(eng, n, i, j):
            pair = n * (NS // 2) + i
            eng.wait_ge(read_out, (pair - 1) * POOL_PAIR + (POOL_PAIR if j else KI) + 2 * KI)
            if j:
                eng.wait_ge(read_out_dve, pair + 2)

        def load(eng, name, signal):
            if name[-1] in "01":
                src = inp[name[:-1]][int(name[-1])]
            else:
                src = inp[name].partition_broadcast(P) if name in ROWS else inp[name]
            if name == "scale_mul":
                src = inp[name][0, :].partition_broadcast(P)
            eng.dma_start(home[name], src).then_inc(signal, 16)

        RES = 4
        x_of = [x_in, x_ssm, x_mlp, x_att, x_out]
        x_rows = inp["x"].rearrange("b (t p) d -> b p t d", p=P)
        out_rows = out.rearrange("b (t p) d -> b p t d", p=P)

        block = ctx.enter_context(nc.Block())

        @block.sync
        def _(sp):
            sp.sem_inc(out_stored, 16)
            for name in FIRST:
                load(sp, name, first_loaded)
            sp.dma_start(x_in[:], x_rows[0]).then_inc(x_loaded, 16)
            load(sp, "in_w0", in0_loaded)
            load(sp, "xproj_w0", xproj0_loaded)
            for name in SSM:
                load(sp, name, ssm_loaded)
            for name in REST:
                load(sp, name, rest_loaded)

            def stack(n):
                sp.wait_ge(bc_ready, (n + 1) * 5)
                for q in range(P // QUAD):
                    for part in range(PARTS):
                        sp.dma_start(bc_stack[part * QUAD:(part + 1) * QUAD, q, :],
                                     bc_parts[q * QUAD:(q + 1) * QUAD, part, :]).then_inc(bc_stacked, 16)

            def turns(b, last):
                stack(b * 2)
                sp.wait_ge(b_tok_mm, b * 2 + 1)
                load(sp, "w12", w12_loaded)
                sp.dma_start(fc1_w[:], inp["fc1_w"]).then_inc(fc1_loaded, 16)
                stack(b * 2 + 1)
                if not last:
                    sp.wait_ge(res_ready, (b * RES + 1) * 2)
                    sp.dma_start(x_in[:], x_rows[b + 1]).then_inc(x_loaded, 16)
                    sp.wait_ge(mlp_mm, (b + 1) * 2 * KH)
                    load(sp, "xproj_w0", xproj0_loaded)
                    sp.wait_ge(fc1_mm, (b + 1) * KF)
                    load(sp, "in_w0", in0_loaded)
                sp.wait_ge(res_ready, (b * RES + RES) * 2)
                sp.dma_start(out_rows[b], x_out[:]).then_inc(out_stored, 16)

            with sp.Fori(0, B - 1) as b:
                turns(b, False)
            turns(B - 1, True)
            sp.wait_ge(out_stored, 16 * (B + 1))

        @block.gpsimd
        def _(pool):
            pool.memset(ident[:], 0.0).then_inc(ident_zero, 1)
            pool.wait_ge(ident_zero, 1)
            pool.affine_select(out=ident[:], in_=ident[:], compare_op=ALU.not_equal, fill=1.0, base=0,
                               pattern=[[-1, P]], channel_multiplier=1).then_inc(ident_ready, 1)
            pool.wait_ge(ident_ready, 1)
            for q in range(PARTS):
                rows = slice(q * QUAD, (q + 1) * QUAD)
                pool.tensor_copy(row_pick[rows, :], ident[rows, rows]).then_inc(ident_ready, 1)
                pool.wait_ge(ident_ready, 2 + q)
            pool.wait_ge(ssm_loaded, 16 * len(SSM))
            for d in range(2):
                for k in range(KI):
                    pool.tensor_scalar(d_diag[:, d, k, :], ident[:], d_skip[:, d, k:k + 1], None,
                                       ALU.mult).then_inc(diag_ready, 1)
            pool.sem_inc(read_out, 2 * KI)
            with pool.Fori(0, B) as b:
                for d in range(2):
                    n = b * 2 + d
                    for u, k in enumerate(ORDER):
                        pool.wait_ge(dt_ready, n * KI + u + 1)
                        pool.tensor_tensor(dtx[:, k, :], dt[:, k, :], xs[:, k, :], ALU.mult).then_inc(dtx_ready, 1)
                    pool.wait_ge(dtx_ready, (n + 1) * KI)
                    pool.sem_inc(wait_over, 1)
                    with pool.Fori(0, NS // 2) as i:
                        for j in range(2):
                            row = n * NS + i * 2 + j
                            pool.wait_ge(c_copied, row + 1 + 1)
                            for k in range(j, KI):
                                pool.wait_ge(scanned, row * KI + k + 1 + CREDIT)
                                pool.wait_ge(summed, (n + row) * KI + k + 1)
                                pool.tensor_tensor(readout[:, k, :], state[:, k, :], c_rows[:, j, :],
                                                   ALU.mult).then_inc(read_out, 1)
                pool.wait_ge(y_ready, (b + 1) * 2 * KI)
                pool.sem_inc(wait_over, 1)
                pool.memset(qk_pad[:], 0.0).then_inc(pads_ready, 1)
                pool.memset(v_ones[:], 1.0).then_inc(ones_ready, 1)
                for t in range(TT):
                    pool.wait_ge(qk_ready, b * TT + t + 1)
                    pool.tensor_tensor(qk_sq[:, t, :], qk[:, t, :], qk[:, t, :], ALU.mult).then_inc(sq_ready, 1)

        @block.scalar
        def _(act):
            act.wait_ge(first_loaded, 16 * len(FIRST))
            act.activation(silu_cond[:], cond[:], ACT.Silu).then_inc(cond_ready, 1)
            act.wait_ge(ssm_loaded, 16 * len(SSM))
            act.activation(a_exp[:], a_log[:], ACT.Exp).then_inc(a_exp_done, 1)
            act.wait_ge(cap_ready, 1)
            act.activation(q_scale[:], scale_cap[:], ACT.Exp).then_inc(q_scale_ready, 1)

            def ln(b, i):
                n = b * 4 + i
                act.wait_ge(ln_var, n + 1)
                act.activation(std[:], var_eps[:], ACT.Sqrt).then_inc(ln_std, 1)
                act.wait_ge(ln_turned, n + 1)
                act.activation(h_t[:, 1, :], banks[1][:], ACT.Identity, bias=mod[:, i, SHIFT, 1, bass.ds(b, 1)],
                               scale=mod[:, i, SCALE, 1, bass.ds(b, 1)]).then_inc(ln_ready, 1)

            act.sem_inc(c_copied, 1)
            act.wait_ge(mod_ready, 2)
            act.wait_ge(gate_ready, 4 * B)
            act.wait_ge(a_ready, 1)
            b_tok_pairs = b_tok[:].rearrange("p t (j i) -> p t j i", j=2)
            a_pairs = a_neg[:].rearrange("p d k (j i) -> p d k j i", j=2)
            with act.Fori(0, B) as b:
                ln(b, 0)
                for d in range(2):
                    n = b * 2 + d
                    for m in range(2 * KI):
                        act.wait_ge(in_mm, n * 2 * KI + m + 1)
                        to = xs[:, m, :] if m < KI else silu_z[:, m - KI, :]
                        act.activation(to, banks[m][:], ACT.Silu).then_inc(in_ready, 1)
                    act.preload_act_table_set("natural_log_exp_and_others")
                    for u, k in enumerate(ORDER):
                        at = n * KI + u + 1
                        act.wait_ge(dt_relu, at)
                        act.activation(log_part[:, k, :], banks[k][:], ACT.Abs,
                                       bias=dt_b[:, d, k:k + 1]).then_inc(dt_abs, 1)
                        act.wait_ge(dt_abs, at)
                        act.activation(log_part[:, k, :], log_part[:, k, :], ACT.Exp, scale=-1.0).then_inc(dt_exp, 1)
                        act.wait_ge(dt_exp, at)
                        act.activation(log_part[:, k, :], log_part[:, k, :], ACT.Ln, bias=1.0).then_inc(dt_log, 1)
                    act.wait_ge(b_tok_mm, n + 1)
                    act.activation(b_tok[:].rearrange("p t s -> p (t s)"), banks[KI + 1][:, 0:TT * NS],
                                   ACT.Copy).then_inc(b_tok_ready, 1)
                    act.wait_ge(dtx_turned, n + 1)
                    act.activation(dtx_tok, banks[3][:].rearrange("p (t c) -> p t c", c=WA),
                                   ACT.Copy).then_inc(dtx_tok_ready, 1)
                    act.wait_ge(b_tok_ready, n + 1)
                    act.wait_ge(dtx_tok_ready, n + 1)
                    act.wait_ge(dt_ready, (n + 1) * KI)
                    if d == 0:
                        act.wait_ge(out_stored, 16 * (b + 1))
                    with act.Fori(0, NS // 2) as i:
                        for j in range(2):
                            row = n * NS + i * 2 + j
                            def decays(channels):
                                for k in channels:
                                    act.wait_ge(scanned, row * KI + k + 1 + CREDIT - RING)
                                    act.activation(decay[:, k, :], dt[:, k, :], ACT.Exp,
                                                   scale=a_pairs[:, d, k, j, bass.ds(i, 1)]).then_inc(decay_ready, 1)

                            decays([0])
                            act.wait_ge(inflow_turned, (row - 2) * KA + TURN_CREDIT)
                            for t in range(TT):
                                act.activation(inflow_tok[j][:, t, :], dtx_tok[:, t, :], ACT.Copy,
                                               scale=b_tok_pairs[:, t, j, bass.ds(i, 1)]).then_inc(inflow_tok_ready, 1)
                            decays([1])
                            act.wait_ge(bc_spread, row + 1)
                            wait_readouts_before(act, n, i, j)
                            act.activation(c_rows[:, j, :], banks[1][:], ACT.Copy).then_inc(c_copied, 1)
                            decays(range(2, KI))
                ln(b, 1)
                for m in range(KH):
                    act.wait_ge(mlp_mm, (b * KH + m) * 2 + 1)
                    act.activation(silu_a[:, m, :], banks[m][:], ACT.Silu).then_inc(mlp_silu, 1)
                ln(b, 2)
                act.wait_ge(norm_sq_ready, (b + 1) * TT)
                act.activation(norm[:], norm_sq[:], ACT.Sqrt).then_inc(norm_ready, 1)
                for i in range(0, 2 * NG, 2):
                    act.wait_ge(qk_turned, b * 2 * NG + i + 1)
                    to = q_t[:, i, :] if i < NG else k_t[:, i - NG, :]
                    act.activation(to, banks[i][:], ACT.Copy).then_inc(qk_t_ready, 1)

                def turned_even(u, i):
                    n = b * STEPS + u
                    act.wait_ge(probs_turned, n * HG + i + 1)
                    if u >= 2:
                        act.wait_ge(pv_mm, n - 1)
                    act.activation(probs_t[u % 2][i], banks[4][:], ACT.Copy).then_inc(probs_t_even, 1)

                def lanes(u):
                    n = b * STEPS + u
                    act.wait_ge(pv_mm, n + 1)
                    if u >= 2:
                        act.wait_ge(lanes_turned, n - 1)
                    act.activation(o_lanes[:, u % 2, :], banks[6][:, 0:P], ACT.Copy).then_inc(lanes_ready, 1)

                for u in range(STEPS):
                    n = b * STEPS + u
                    for i in range(HG):
                        act.wait_ge(neg_ready, n * HG + i + 1)
                        if u:
                            act.wait_ge(probs_turned, (n - 1) * HG + i + 1)
                        act.activation(probs[:, i, :], banks[i][:], ACT.Exp, scale=-1.0,
                                       bias=neg_max[:, u % 2, i:i + 1]).then_inc(probs_ready, 1)
                        if u and i % 2 == 0:
                            turned_even(u - 1, i)
                        if u >= 2 and i == 2:
                            lanes(u - 2)
                for i in range(0, HG, 2):
                    turned_even(STEPS - 1, i)
                lanes(STEPS - 2)
                lanes(STEPS - 1)
                act.wait_ge(o_turned, b + 1)
                act.activation(o_t[:, 1, :], banks[1][:], ACT.Copy).then_inc(o_t_ready, 1)
                ln(b, 3)
                for m in range(KF):
                    act.wait_ge(fc1_mm, b * KF + m + 1)
                    act.activation(gelu_h[:, m, :], banks[m][:], ACT.Gelu, bias=fc1_b[:, m:m + 1]).then_inc(fc1_ready, 1)

        @block.tensor
        def _(pe):
            pe.wait_ge(ident_ready, 1 + PARTS)
            pe.wait_ge(first_loaded, 16 * len(FIRST))
            pe.wait_ge(cond_ready, 1)
            pe.sem_inc(inflow_turned, TURN_CREDIT)
            for i in range(4):
                c = cond if i < 2 else silu_cond
                for w in range(2):
                    for f in range(KD):
                        at = ((i * 2 + w) * KD + f) * B
                        for kc in range(KD):
                            last = pe.matmul(banks[0][:, at:at + B], mod_w[:, kc, i, w, f * P:(f + 1) * P], c[:, kc, :],
                                             start=(kc == 0), stop=(kc == KD - 1))
            last.then_inc(mod_mm, 1)
            for b in range(B):
                for g in range(4):
                    c = cond if g < 2 else silu_cond
                    u = b * 4 + g
                    if u >= 4:
                        pe.wait_ge(gate_ready, u - 3)
                    for kc in range(KD):
                        last = pe.matmul(banks[1 + u % 4][:, 0:D], c[:, kc, b:b + 1].to_broadcast([P, P]),
                                         gate_w[:, kc, g, :], start=(kc == 0), stop=(kc == KD - 1))
                    last.then_inc(gate_mm, 1)
            pe.wait_ge(gate_ready, 4 * B)
            pe.wait_ge(mod_ready, 2)
            pe.wait_ge(ssm_loaded, 16 * len(SSM))
            pe.wait_ge(diag_ready, 2 * KI)
            def ln(b, i):
                n = b * 4 + i
                for t in range(TT):
                    pe.wait_ge(ln_norm, n * TT + t + 1)
                    for f in range(KD):
                        last = pe.transpose(banks[f][:, t * P:(t + 1) * P], x_norm[:, t, f * P:(f + 1) * P], ident[:])
                last.then_inc(ln_turned, 1)
                pe.wait_ge(ln_ready, (n + 1) * KD)

            def spread(n, i, j):
                row = n * NS + i * 2 + j
                pe.wait_ge(inflow_ready, (row - 1) * KV + FLOW_CREDIT)
                pe.wait_ge(c_copied, row + 1)
                pick = row_pick[:, bass.ds(i, 1)].to_broadcast([PARTS * QUAD, P])
                for c in range(2):
                    last = pe.matmul(banks[1 if c else 2 * j][:], pick, bc_stack[:, c * NS // QUAD + j, :], start=True, stop=True)
                last.then_inc(bc_spread, 1)

            def turn_inflow(n, i, j, k):
                row = n * NS + i * 2 + j
                pe.wait_ge(inflow_tok_ready, (row + 1) * TT)
                pe.wait_ge(scanned, (row - 1) * KI + k + 1 + CREDIT)
                for t in range(TT):
                    last = pe.transpose(banks[k][:, t * P:(t + 1) * P], inflow_tok[j][:, t, (k - KV) * P:(k - KV + 1) * P],
                                        ident[:])
                last.then_inc(inflow_turned, 1)

            def sums(n, i, j, channels):
                for k in channels:
                    wait_readout(pe, n, i, j, k)
                    pe.matmul(banks[4 + k][:], ident[:], readout[:, k, :], start=False, stop=True,
                              skip_group_check=True).then_inc(summed, 1)

            def row_step(n, i, j, following=None, after=None):
                sums(n, i, j, range(KV - 1))
                for k in range(KV, KI):
                    sums(n, i, j, [k - 1])
                    if following:
                        turn_inflow(n, *following, k)
                if after:
                    spread(n, *after)
                sums(n, i, j, [KI - 1])

            def residual_rows(lhs, rhs, steps):
                for t in range(TT):
                    for c in range(steps):
                        last = pe.matmul(banks[t // 2][:, (t % 2) * D:(t % 2 + 1) * D], lhs(c, t), rhs(c),
                                         start=(c == 0), stop=(c == steps - 1))
                    if t % 2:
                        last.then_inc(res_mm, 1)

            with pe.Fori(0, B) as b:
                ln(b, 0)
                for d in range(2):
                    n = b * 2 + d
                    if d == 0:
                        pe.wait_ge(in0_loaded, 16 * (b + 1))
                        pe.wait_ge(xproj0_loaded, 16 * (b + 1))
                    for m in range(2 * KI):
                        if d == 1 and m >= KI:
                            pe.wait_ge(y_ready, (n - 1) * KI + m - KI + 1)
                        for kc in range(KD):
                            last = pe.matmul(banks[m][:], in_w[d][:, kc, m * P:(m + 1) * P], h_t[:, kc, :],
                                             start=(kc == 0), stop=(kc == KD - 1))
                        last.then_inc(in_mm, 1)
                    pe.wait_ge(in_ready, (n + 1) * 2 * KI)
                    for m in [KI] + ORDER:
                        for kc in range(KI):
                            last = pe.matmul(banks[m][:], xproj_w[d][:, kc, m * P:(m + 1) * P], xs[:, kc, :],
                                             start=(kc == 0), stop=(kc == KI - 1))
                        last.then_inc(xproj_mm, 1)
                    for t in range(TT):
                        for kc in range(KI):
                            last = pe.matmul(banks[KI + 1][:, t * NS:(t + 1) * NS], xs[:, kc, t * P:(t + 1) * P],
                                             xproj_w[d][:, kc, DI:DI + NS], start=(kc == 0), stop=(kc == KI - 1))
                    last.then_inc(b_tok_mm, 1)
                    pe.wait_ge(dtx_ready, n * KI + KA)
                    pe.wait_ge(dt_abs, (n + 1) * KI)
                    for t in range(TT):
                        for k in range(KV, KI):
                            at = t * WA + (k - KV) * P
                            last = pe.transpose(banks[3][:, at:at + P], dtx[:, k, t * P:(t + 1) * P], ident[:])
                    last.then_inc(dtx_turned, 1)
                    pe.wait_ge(bc_ready, (n + 1) * 5)
                    pe.wait_ge(b_tok_ready, n + 1)
                    for k in range(KI):
                        pe.matmul(banks[4 + k][:], d_diag[:, d, k, :], xs[:, k, :], start=True,
                                  stop=True).then_inc(summed, 1)
                    pe.wait_ge(bc_stacked, (n + 1) * 16 * PARTS * P // QUAD)
                    spread(n, 0, 0)
                    spread(n, 0, 1)
                    for k in range(KV, KI):
                        turn_inflow(n, 0, 0, k)
                    with pe.Fori(0, NS // 2 - 1) as i:
                        row_step(n, i, 0, (i, 1), (i + 1, 0))
                        row_step(n, i, 1, (i + 1, 0), (i + 1, 1))
                    row_step(n, NS // 2 - 1, 0, (NS // 2 - 1, 1))
                    row_step(n, NS // 2 - 1, 1)
                for d in range(2):
                    for k in range(KI):
                        if d == 1:
                            pe.wait_ge(y_ready, (b * 2 + 1) * KI + k + 1)
                        for t in range(TT):
                            last = pe.matmul(banks[t][:, 0:D], y_gated[:, d, k, t * P:(t + 1) * P], out_w[:, d, k, :],
                                             start=(d == 0 and k == 0), stop=(d == 1 and k == KI - 1))
                            if d == 1 and k == KI - 1 and t % 2:
                                last.then_inc(res_mm, 1)
                ln(b, 1)
                pe.wait_ge(rest_loaded, 16 * len(REST))
                pe.wait_ge(w12_loaded, 16 * (b + 1))
                for m in range(KH):
                    for w in range(2):
                        for kc in range(KD):
                            last = pe.matmul(banks[m + w * KH][:], w12[:, w, kc, m * P:(m + 1) * P], h_t[:, kc, :],
                                             start=(kc == 0), stop=(kc == KD - 1))
                        last.then_inc(mlp_mm, 1)
                pe.wait_ge(mlp_ready, (b + 1) * KH)
                residual_rows(lambda c, t: ab[:, c, t * P:(t + 1) * P], lambda c: w3[:, c, :], KH)
                ln(b, 2)
                for t in range(TT):
                    for kc in range(KD):
                        pe.matmul(banks[t][:], h_t[:, kc, t * P:(t + 1) * P], qkv_w[:, kc, 0:2 * D],
                                  start=(kc == 0), stop=(kc == KD - 1))
                    for kc in range(KD):
                        last = pe.matmul(banks[4 + t][:, 0:D], h_t[:, kc, t * P:(t + 1) * P], qkv_w[:, kc, 2 * D:3 * D],
                                         start=(kc == 0), stop=(kc == KD - 1))
                    last.then_inc(qkv_mm, 1)
                pe.wait_ge(v_ready, (b + 1) * TT)
                for i in range(2 * NG):
                    for t in range(TT):
                        pe.wait_ge(qk_unit, b * TT + t + 1)
                        last = pe.transpose(banks[i][:, t * P:(t + 1) * P], qk_pad[:, t, i, :], ident[:])
                    last.then_inc(qk_turned, 1)
                pe.wait_ge(qk_t_ready, (b + 1) * 2 * NG)

                def scores(u, i):
                    n = b * STEPS + u
                    t, g = u // NG, u % NG
                    if u:
                        pe.wait_ge(probs_ready, (n - 1) * HG + i + 1)
                    a = slice(i * LANE, (i + 1) * LANE)
                    pe.matmul(banks[i][:], q_t[a, g, t * P:(t + 1) * P], k_t[a, g, :], start=True,
                              stop=True).then_inc(scores_mm, 1)

                def turn(u, i):
                    n = b * STEPS + u
                    pe.wait_ge(probs_ready, n * HG + i + 1)
                    if u or i >= 2:
                        pe.wait_ge((probs_t_even, probs_t_odd)[i % 2], n * 2 + i // 2)
                    for kt in range(TT):
                        last = pe.transpose(banks[4 + i % 2][:, kt * P:(kt + 1) * P],
                                            probs[:, i, kt * P:(kt + 1) * P], ident[:])
                    last.then_inc(probs_turned, 1)

                def weigh(u):
                    n = b * STEPS + u
                    g = u % NG
                    pe.wait_ge(probs_t_even, (n + 1) * 2)
                    pe.wait_ge(probs_t_odd, (n + 1) * 2)
                    if u:
                        pe.wait_ge(lanes_ready, n)
                    for kt in range(TT):
                        for i in range(HG):
                            last = pe.matmul(banks[6][i * LANE:(i + 1) * LANE, 0:P], v_ones[:, kt, g * HG + i, :],
                                             probs_t[u % 2][i][:, kt * P:(kt + 1) * P], start=(kt == 0),
                                             stop=(kt == TT - 1), tile_position=(0, i * LANE))
                    last.then_inc(pv_mm, 1)

                def turn_back(u):
                    n = b * STEPS + u
                    pe.wait_ge(lanes_ready, n + 1)
                    if u:
                        pe.wait_ge(o_ready, n)
                    pe.transpose(banks[7][:, 0:P], o_lanes[:, u % 2, :], ident[:]).then_inc(lanes_turned, 1)

                for i in range(HG):
                    scores(0, i)
                for u in range(STEPS):
                    for i in range(HG):
                        if u + 1 < STEPS:
                            scores(u + 1, i)
                        turn(u, i)
                        if i == 1 and u:
                            weigh(u - 1)
                            if u >= 2:
                                turn_back(u - 2)
                weigh(STEPS - 1)
                turn_back(STEPS - 2)
                turn_back(STEPS - 1)
                pe.wait_ge(o_ready, (b + 1) * STEPS)
                for t in range(TT):
                    for f in range(KD):
                        last = pe.transpose(banks[f][:, t * P:(t + 1) * P], o_rows[:, t, f * P:(f + 1) * P], ident[:])
                last.then_inc(o_turned, 1)
                pe.wait_ge(o_t_ready, (b + 1) * KD)
                residual_rows(lambda c, t: o_t[:, c, t * P:(t + 1) * P], lambda c: proj_w[:, c, :], KD)
                ln(b, 3)
                pe.wait_ge(fc1_loaded, 16 * (b + 1))
                for m in range(KF):
                    for kc in range(KD):
                        last = pe.matmul(banks[m][:], fc1_w[:, kc, m * P:(m + 1) * P], h_t[:, kc, :],
                                         start=(kc == 0), stop=(kc == KD - 1))
                    last.then_inc(fc1_mm, 1)
                pe.wait_ge(fc1_ready, (b + 1) * KF)
                residual_rows(lambda c, t: gelu_h[:, c, t * P:(t + 1) * P], lambda c: fc2_w[:, c, :], KF)

        @block.vector
        def _(dve):
            dve.wait_ge(first_loaded, 16 * len(FIRST))
            dve.wait_ge(mod_mm, 1)
            dve.tensor_tensor(mod[:].rearrange("p i w f b -> p (i w f) b"),
                              banks[0][:, 0:16 * B].rearrange("p (g b) -> p g b", b=B),
                              mod_b[:].rearrange("p i w f -> p (i w f)").unsqueeze(2).to_broadcast([P, 16, B]),
                              ALU.add).then_inc(mod_sum, 1)
            dve.wait_ge(mod_sum, 1)
            one_plus = mod[:, :, SCALE, :, :].rearrange("p i f b -> p i (f b)")
            dve.tensor_scalar(one_plus, one_plus, 1.0, None, ALU.add).then_inc(mod_ready, 2)
            for b in range(B):
                for g in range(4):
                    u = b * 4 + g
                    dve.wait_ge(gate_mm, u + 1)
                    dve.tensor_tensor(gate[:, b, g, :], banks[1 + u % 4][:, 0:D], gate_b[:, g, :],
                                      ALU.add).then_inc(gate_ready, 1)
            dve.wait_ge(a_exp_done, 1)
            dve.tensor_scalar(a_neg[:], a_exp[:], -1.0, None, ALU.mult).then_inc(a_ready, 1)
            dve.wait_ge(rest_loaded, 16 * len(REST))
            dve.tensor_scalar(scale_cap[:], scale_mul[:], MAX_SCALE_MUL, None, ALU.min).then_inc(cap_ready, 1)
            dve.wait_ge(gate_ready, 4 * B)
            dve.wait_ge(mod_ready, 2)
            dve.wait_ge(q_scale_ready, 1)
            dve.sem_inc(inflow_ready, FLOW_CREDIT)
            dve.sem_inc(scanned, CREDIT)
            dve.sem_inc(read_out_dve, 2)

            def ln(b, i, x, eps):
                n = b * 4 + i
                for t in range(TT if i == 0 else 0):
                    dve.bn_stats(stats[:, t, :], x[:, t, :]).then_inc(ln_stat, 1)
                dve.wait_ge(ln_stat, (n + 1) * TT)
                dve.sem_inc(wait_over, 1)
                for t in range(TT):
                    dve.bn_aggr(mean_var[:, t, :], stats[:, t, :]).then_inc(ln_aggr, 1)
                dve.wait_ge(ln_aggr, (n + 1) * TT)
                dve.tensor_scalar(var_eps[:], mean_var[:, :, 1], eps, None, ALU.add).then_inc(ln_var, 1)
                dve.wait_ge(ln_std, n + 1)
                dve.reciprocal(rstd[:], std[:]).then_inc(ln_rstd, 1)
                dve.wait_ge(ln_rstd, n + 1)
                for t in range(TT):
                    dve.tensor_scalar(x_norm[:, t, :], x[:, t, :], mean_var[:, t, 0:1], rstd[:, t:t + 1],
                                      ALU.subtract, ALU.mult).then_inc(ln_norm, 1)
                dve.wait_ge(ln_turned, n + 1)
                dve.tensor_scalar(h_t[:, 0, :], banks[0][:], mod[:, i, SCALE, 0, bass.ds(b, 1)], mod[:, i, SHIFT, 0, bass.ds(b, 1)],
                                  ALU.mult, ALU.add).then_inc(ln_ready, 1)

            def add_up(b, i, n, tiles):
                dve.wait_ge(res_gated, n + 1)
                dve.tensor_tensor(x_of[i + 1][:, tiles, :], x_of[i][:, tiles, :], gated[:, tiles, :],
                                  ALU.add).then_inc(res_ready, 1)
                if i + 1 < RES:
                    dve.wait_ge(res_ready, n + 1)
                    for t in range(tiles.start, tiles.stop):
                        dve.bn_stats(stats[:, t, :], x_of[i + 1][:, t, :]).then_inc(ln_stat, 1)

            def residual(b, i, g, bias=None):
                for p in range(2):
                    n = (b * RES + i) * 2 + p
                    tiles = slice(2 * p, 2 * p + 2)
                    dve.wait_ge(res_mm, n + 1)
                    if i == 0:
                        for t in range(2 * p, 2 * p + 2):
                            last = dve.tensor_tensor(gated[:, t, :], banks[t][:, 0:D], gate[:, b, g, :], ALU.mult)
                        last.then_inc(res_gated, 1)
                        add_up(b, i, n, tiles)
                        continue
                    src = banks[p][:].rearrange("p (t d) -> p t d", d=D)
                    if bias is not None:
                        dve.tensor_tensor(biased[:, tiles, :], src, row_b[:, bias:bias + 1, :].to_broadcast([P, 2, D]),
                                          ALU.add).then_inc(res_biased, 1)
                        dve.wait_ge(res_biased, b * 4 + (2 if i == 3 else 0) + p + 1)
                        src = biased[:, tiles, :]
                    dve.tensor_tensor(gated[:, tiles, :], src, gate[:, b, g, :].unsqueeze(1).to_broadcast([P, 2, D]),
                                      ALU.mult).then_inc(res_gated, 1)
                    add_up(b, i, n, tiles)

            def add_log(n, u):
                k = ORDER[u]
                dve.wait_ge(dt_relu, n * KI + u + 1)
                dve.wait_ge(dt_log, n * KI + u + 1)
                dve.tensor_tensor(dt[:, k, :], dt[:, k, :], log_part[:, k, :], ALU.add).then_inc(dt_ready, 1)

            with dve.Fori(0, B) as b:
                dve.wait_ge(x_loaded, (b + 1) * 16)
                ln(b, 0, x_in, EPS_MAMBA)
                for d in range(2):
                    n = b * 2 + d
                    at = n * (KI + 1) + 1
                    dve.wait_ge(xproj_mm, at)
                    dve.tensor_copy(bc_parts[:, 0, :], banks[KI][:]).then_inc(bc_ready, 1)
                    dve.wait_ge(bc_ready, n * 5 + 1)
                    dve.tensor_tensor(bc_rest[:], banks[KI][:], bc_parts[:, 0, :], ALU.subtract).then_inc(bc_ready, 1)
                    dve.wait_ge(bc_ready, n * 5 + 2)
                    dve.tensor_copy(bc_parts[:, 1, :], bc_rest[:]).then_inc(bc_ready, 1)
                    dve.wait_ge(bc_ready, n * 5 + 3)
                    dve.tensor_tensor(bc_rest[:], bc_rest[:], bc_parts[:, 1, :], ALU.subtract).then_inc(bc_ready, 1)
                    dve.wait_ge(bc_ready, n * 5 + 4)
                    dve.tensor_copy(bc_parts[:, 2, :], bc_rest[:]).then_inc(bc_ready, 1)
                    for u, k in enumerate(ORDER):
                        dve.wait_ge(xproj_mm, at + u + 1)
                        dve.tensor_scalar(dt[:, k, :], banks[k][:], dt_b[:, d, k:k + 1], 0.0,
                                          ALU.add, ALU.max).then_inc(dt_relu, 1)
                        if u:
                            add_log(n, u - 1)
                    add_log(n, KI - 1)
                    dve.wait_ge(dtx_ready, (n + 1) * KI)
                    dve.sem_inc(wait_over, 1)
                    time = slice(None, None, -1) if d else slice(None)

                    def inflow_of(row, j, k):
                        dve.wait_ge(scanned, (row - 1) * KI + k + 1 + CREDIT)
                        dve.tensor_tensor(inflow[:, k, :], dtx[:, k, :], banks[2 * j][:], ALU.mult).then_inc(inflow_ready, 1)

                    def read_first(row):
                        dve.wait_ge(scanned, row * KI + 1 + CREDIT)
                        dve.wait_ge(c_copied, row + 1 + 1)
                        dve.wait_ge(summed, (n + row) * KI + 1)
                        dve.tensor_tensor(readout[:, 0, :], state[:, 0, :], c_rows[:, 1, :], ALU.mult).then_inc(read_out_dve, 1)

                    def scan(row, i, j, k):
                        dve.wait_ge(decay_ready, row * KI + k + 1)
                        if k < KV:
                            dve.wait_ge(inflow_ready, row * KV + k + 1 + FLOW_CREDIT)
                        else:
                            dve.wait_ge(inflow_turned, row * KA + k - KV + 1 + TURN_CREDIT)
                        if j:
                            wait_readout(dve, n, i, 0, k)
                        else:
                            wait_readout(dve, n, i - 1, 1, k)
                        source = inflow[:, k, time] if k < KV else banks[k][:, time]
                        dve.tensor_tensor_scan(state[:, k, time], decay[:, k, time], source, 0.0,
                                               ALU.mult, ALU.add).then_inc(scanned, 1)

                    with dve.Fori(0, NS // 2) as i:
                        for j in range(2):
                            row = n * NS + i * 2 + j
                            dve.wait_ge(bc_spread, row + 1)
                            inflow_of(row, j, 0)
                            for k in range(KI):
                                if k + 1 < KV:
                                    inflow_of(row, j, k + 1)
                                scan(row, i, j, k)
                                if j and k == 1:
                                    read_first(row)
                    for k in range(KI):
                        dve.wait_ge(summed, ((n + 1) * (NS + 1) - 1) * KI + k + 1)
                        dve.tensor_tensor(y_gated[:, d, k, :], banks[4 + k][:], silu_z[:, k, :],
                                          ALU.mult).then_inc(y_ready, 1)
                residual(b, 0, GATE_MAMBA)
                ln(b, 1, x_ssm, EPS_MAMBA)
                dve.wait_ge(out_stored, 16 * (b + 1))
                for m in range(KH):
                    dve.wait_ge(mlp_silu, b * KH + m + 1)
                    dve.wait_ge(mlp_mm, (b * KH + m + 1) * 2)
                    dve.tensor_tensor(ab[:, m, :], banks[4 + m][:], silu_a[:, m, :], ALU.mult).then_inc(mlp_ready, 1)
                residual(b, 1, GATE_MLP)
                ln(b, 2, x_mlp, EPS_LN)
                dve.wait_ge(ones_ready, b + 1)
                def sum_squares(t):
                    dve.wait_ge(sq_ready, b * TT + t + 1)
                    dve.tensor_reduce(norm_sq[:, t, :], qk_sq[:, t, :].rearrange("p (h e) -> p h e", e=HD), AX.X,
                                      ALU.add).then_inc(norm_sq_ready, 1)

                for t in range(TT):
                    dve.wait_ge(qkv_mm, b * TT + t + 1)
                    dve.tensor_tensor(qk[:, t, 0:D], banks[t][:, 0:D], row_b[:, Q_BIAS, :], ALU.add)
                    dve.tensor_copy(qk[:, t, D:2 * D], banks[t][:, D:2 * D]).then_inc(qk_ready, 1)
                    dve.tensor_tensor(v_ones[:, t, :, 0:HD], banks[4 + t][:, 0:D].rearrange("p (h e) -> p h e", e=HD),
                                      row_b[:, V_BIAS, :].rearrange("p (h e) -> p h e", e=HD),
                                      ALU.add).then_inc(v_ready, 1)
                    if t:
                        sum_squares(t - 1)
                sum_squares(TT - 1)
                dve.wait_ge(norm_ready, b + 1)
                dve.tensor_scalar(norm_max[:], norm[:], EPS_NORM, None, ALU.max).then_inc(norm_max_ready, 1)
                dve.wait_ge(norm_max_ready, b + 1)
                dve.reciprocal(norm_inv[:], norm_max[:]).then_inc(norm_inv_ready, 1)
                dve.wait_ge(norm_inv_ready, b + 1)
                dve.tensor_tensor(norm_inv[:, :, 0:H], norm_inv[:, :, 0:H],
                                  q_scale[:].unsqueeze(1).to_broadcast([P, TT, H]), ALU.mult).then_inc(q_inv_ready, 1)
                dve.tensor_scalar(norm_inv[:, :, H:2 * H], norm_inv[:, :, H:2 * H], -1.0, None,
                                  ALU.mult).then_inc(q_inv_ready, 1)
                dve.wait_ge(q_inv_ready, (b + 1) * 2)
                dve.wait_ge(pads_ready, b + 1)
                for t in range(TT):
                    pad = qk_pad[:, t, :, :].rearrange("p g (h e) -> p (g h) e", e=LANE)
                    dve.tensor_tensor(pad[:, :, 0:HD], qk[:, t, :].rearrange("p (h e) -> p h e", e=HD),
                                      norm_inv[:, t, :].unsqueeze(2).to_broadcast([P, 2 * H, HD]),
                                      ALU.mult).then_inc(qk_unit, 1)
                for i in range(1, 2 * NG, 2):
                    dve.wait_ge(qk_turned, b * 2 * NG + i + 1)
                    to = q_t[:, i, :] if i < NG else k_t[:, i - NG, :]
                    dve.tensor_copy(to, banks[i][:]).then_inc(qk_t_ready, 1)

                def least(u, i):
                    n = b * STEPS + u
                    dve.wait_ge(scores_mm, n * HG + i + 1)
                    dve.tensor_reduce(neg_max[:, u % 2, i:i + 1], banks[i][:], AX.X, ALU.min).then_inc(neg_ready, 1)

                def turned_odd(u, i):
                    n = b * STEPS + u
                    dve.wait_ge(probs_turned, n * HG + i + 1)
                    if u >= 2:
                        dve.wait_ge(pv_mm, n - 1)
                    dve.tensor_copy(probs_t[u % 2][i], banks[5][:]).then_inc(probs_t_odd, 1)

                def divide(u):
                    n = b * STEPS + u
                    t, g = u // NG, u % NG
                    o = banks[7][:, 0:P].rearrange("p (i e) -> p i e", e=LANE)
                    dve.wait_ge(lanes_turned, n + 1)
                    dve.reciprocal(sum_inv[:, u % 2, :], o[:, :, HD]).then_inc(sum_inv_ready, 1)
                    dve.wait_ge(sum_inv_ready, n + 1)
                    dve.tensor_tensor(o_rows[:, t, g * HG * HD:(g + 1) * HG * HD].rearrange("p (i e) -> p i e", e=HD),
                                      o[:, :, 0:HD], sum_inv[:, u % 2, :].unsqueeze(2).to_broadcast([P, HG, HD]),
                                      ALU.mult).then_inc(o_ready, 1)

                for i in range(HG):
                    least(0, i)
                for u in range(STEPS):
                    for i in range(HG):
                        if u + 1 < STEPS:
                            least(u + 1, i)
                        if i % 2:
                            turned_odd(u, i)
                    if u >= 2:
                        divide(u - 2)
                divide(STEPS - 2)
                divide(STEPS - 1)
                dve.wait_ge(o_turned, b + 1)
                dve.tensor_copy(o_t[:, 0, :], banks[0][:]).then_inc(o_t_ready, 1)
                residual(b, 2, GAMMA1, PROJ_B)
                ln(b, 3, x_att, EPS_LN)
                residual(b, 3, GAMMA2, FC2_B)


def kernel(**inputs):
    import numpy as np
    import concourse.bacc as bacc
    from concourse.bass_utils import run_bass_kernel_spmd

    a = {k: np.asarray(v) for k, v in inputs.items()}

    def cut(w):
        return w.reshape(-1, P, *w.shape[1:]).swapaxes(0, 1)

    mamba_w, mlp_w, ada_w = a["L0_cond_adaln_mamba_w"], a["L0_cond_adaln_mlp_w"], a["L1_cond_ada_w"].T
    mamba_b, mlp_b, ada_b = a["L0_cond_adaln_mamba_b"], a["L0_cond_adaln_mlp_b"], a["L1_cond_ada_b"]

    def col(w, i):
        return w[..., i * D:(i + 1) * D]

    pairs_w = [(col(mamba_w, 0), col(mamba_w, 1)), (col(mlp_w, 0), col(mlp_w, 1)),
               (col(ada_w, 4), col(ada_w, 2)), (col(ada_w, 5), col(ada_w, 3))]
    pairs_b = [(col(mamba_b, 0), col(mamba_b, 1)), (col(mlp_b, 0), col(mlp_b, 1)),
               (col(ada_b, 4), col(ada_b, 2)), (col(ada_b, 5), col(ada_b, 3))]
    gates_w = [col(mamba_w, 2), col(mlp_w, 2), col(ada_w, 0), col(ada_w, 1)]
    gates_b = [col(mamba_b, 2), col(mlp_b, 2), col(ada_b, 0), col(ada_b, 1)]

    def both(name):
        return np.stack([cut(a[f"L0_cond_{d}_{name}"]) for d in ("fwd", "bwd")], 1)

    laid = {
        "x": a["x"],
        "cond": cut(a["cond_1024"].T),
        "mod_w": cut(np.stack([np.stack(p, 1) for p in pairs_w], 1)),
        "mod_b": np.stack([np.stack([v.reshape(KD, P).T for v in p], 1) for p in pairs_b], 1),
        "gate_w": cut(np.stack(gates_w, 1)),
        "gate_b": np.stack(gates_b, 0),
        "in_w": both("in_w").swapaxes(0, 1),
        "xproj_w": both("xproj_w").swapaxes(0, 1),
        "dt_b": both("dt_bias"),
        "a_log": both("A_log"),
        "d_skip": both("D"),
        "out_w": both("out_w"),
        "w12": np.stack([cut(a["L0_cond_mlp_w1"]), cut(a["L0_cond_mlp_w2"])], 1),
        "w3": cut(a["L0_cond_mlp_w3"]),
        "qkv_w": cut(a["L1_cond_mat_qkv_w"].T),
        "row_b": np.stack([a[f"L1_cond_{v}"] for v in ("q_bias", "v_bias", "proj_b", "fc2_b")], 0),
        "scale_mul": a["L1_cond_scale_mul"].reshape(1, H),
        "proj_w": cut(a["L1_cond_proj_w"].T),
        "fc1_w": cut(a["L1_cond_fc1_w"].T),
        "fc1_b": cut(a["L1_cond_fc1_b"]),
        "fc2_w": cut(a["L1_cond_fc2_w"].T),
    }
    nc = bacc.Bacc("TRN2", target_bir_lowering=False, num_devices=1)
    arrays, aps = {}, {}
    for name, shape in INPUTS.items():
        arrays[f"in_{name}"] = np.ascontiguousarray(laid[name]).reshape(shape)
        aps[name] = nc.dram_tensor(f"in_{name}", shape, F32, kind="ExternalInput").ap()
    out = nc.dram_tensor("out", [B, L, D], F32, kind="ExternalOutput").ap()
    build(nc, aps, out)
    r = run_bass_kernel_spmd(nc, [arrays], core_ids=[0])
    return r.results[0]["out"]
```
